# Optimizing a Trainium2 kernel written in Bass

```python
import numpy as np
import jax
import jax.numpy as jnp

def _softmax(x, axis=-1):
    return jax.nn.softmax(x, axis=axis)

def _gelu(x):
    return jax.nn.gelu(x, approximate=True)

def _silu(x):
    return jax.nn.silu(x)

def _sigmoid(x):
    return jax.nn.sigmoid(x)

def _layernorm(x, axis=-1, eps=1e-05):
    m = jnp.mean(x, axis=axis, keepdims=True)
    v = jnp.var(x, axis=axis, keepdims=True)
    return (x - m) / jnp.sqrt(v + eps)

def _scatter_add(tgt, idx, src, axis=0):
    return tgt.at[idx].add(src)

def _segment_sum(src, seg, n):
    return jax.ops.segment_sum(src, seg, n)
kernel_name = 'mk_adj_preln_d1_adj_r2_c5be2c'

def setup_inputs(seed: int=0):
    np.random.seed(seed)
    _w = jnp.asarray

    def _rec_inputs():
        import jax
        import jax.numpy as jnp
        _gk = jax.random.key(seed)
        x = -0.0005146 + 1 * jax.random.normal(jax.random.fold_in(_gk, 1), (8, 1024, 128), jnp.float32)
        _w = (1.0 + jnp.arange(1024, dtype=jnp.float32)) ** (-0.5)
        _w = _w / _w.mean()
        _pij = jnp.clip(0.015625 * _w[:, None] * _w[None, :], 0.0, 1.0)
        _a = jax.random.uniform(jax.random.fold_in(_gk, 2), (8, 1024, 1024)) < _pij
        adj = _a.astype(jnp.int32)
        return (x, adj)
    x, adj = _rec_inputs()

    def _L0_gnn_setup():
        import jax, jax.numpy as jnp
        import numpy as np
        B, N, C, OUT, S = (4, 1024, 128, 128, 25)
        DENSITY = 0.008
        key = jax.random.key(seed)
        kA, kX, kW = jax.random.split(key, 3)
        A = jax.random.bernoulli(kA, DENSITY, (B, N, N)).astype(jnp.int32)
        X = jax.random.normal(kX, (B, N, C), dtype=jnp.float32)
        W = jax.random.normal(kW, (2 * C, OUT), dtype=jnp.float32) * np.float32(1.0 / np.sqrt(2 * C))
        b = jnp.zeros((OUT,), dtype=jnp.float32)
        return {'A': A, 'X': X, 'W': W, 'b': b}
    _L0_gnn_all = _L0_gnn_setup()
    _L0_gnn_in = {k: v for k, v in _L0_gnn_all.items() if k in ('W', 'b')}
    del _L0_gnn_all
    return {'x': x, 'adj': adj, 'L0_gnn_W': _L0_gnn_in['W'], 'L0_gnn_b': _L0_gnn_in['b']}

def reference(x, adj, L0_gnn_W, L0_gnn_b):
    import jax
    import jax.numpy as jnp

    def _L0_gnn_ref(A, X, W, b):
        import jax, jax.numpy as jnp
        import numpy as np
        B, N, C, OUT, S = (4, 1024, 128, 128, 25)
        DENSITY = 0.008
        mask = A != 0
        neg_inf = jnp.float32(-jnp.inf)
        pri = -jnp.arange(N, dtype=jnp.float32)
        scores = jnp.where(mask, pri, neg_inf)
        vals, idx = jax.lax.top_k(scores, S)
        valid = vals > neg_inf
        feats = jax.vmap(lambda x, i: x[i])(X, idx)
        feats = jnp.where(valid[..., None], feats, neg_inf)
        agg = feats.max(axis=2)
        degree = mask.sum(axis=-1)
        agg = jnp.where((degree <= S)[..., None], jnp.maximum(agg, 0.0), agg)
        h = jnp.concatenate([X, agg], axis=-1)
        out = jax.nn.relu(jnp.einsum('bnf,fo->bno', h, W) + b)
        return out
    h = jnp.maximum(_layernorm(x, axis=-1), 0.0)
    x = x + _L0_gnn_ref(adj, h, L0_gnn_W, L0_gnn_b)
    return x

_drawn_inputs = setup_inputs


def setup_inputs(seed=0):
    import zlib

    import numpy as np

    out = dict(_drawn_inputs(seed))
    spreads = {'L0_gnn_b': (0.0, 0.1)}
    factors = {}
    for name, (base, spread) in spreads.items():
        noise = np.random.default_rng([zlib.crc32(name.encode()), seed]).standard_normal(out[name].shape)
        drawn = base * np.exp(spread * noise) if base else spread * noise
        out[name] = jnp.asarray(drawn.astype(out[name].dtype))
    for name, factor in factors.items():
        out[name] = (out[name] * factor).astype(out[name].dtype)
    return out
```

```python
from contextlib import ExitStack

import concourse.bass as bass
from concourse import mybir

F32 = mybir.dt.float32
F16 = mybir.dt.float16
BF16 = mybir.dt.bfloat16
I32 = mybir.dt.int32
ALU = mybir.AluOpType
ACT = mybir.ActivationFunctionType
AX = mybir.AxisListType

P = 128
NEIGHBOURS = 25
BASE = 5
EPS = 1e-5
SCALE = 4096.0
BIG = 128.0


def build(nc, x, adj, W, b, out):
    B, N, C = x.shape
    K = N // P
    ROWS = 512
    Q = ROWS // P
    GROUPS = B * N // ROWS
    PER_BATCH = N // ROWS
    UNROLL = 2 * PER_BATCH
    ITERS = GROUPS // UNROLL
    PAIRS = K // 2
    HALF = K // 2
    T_USES, STAGE_USES = K // 2, K
    RING = T_USES + 3 * STAGE_USES
    assert C == P and K == 8 and PER_BATCH == 2 and BASE >= 3 and RING % 2 == 0

    adj_v = adj.rearrange("b (h p q) j -> (b h) p (q j)", p=P, q=Q)
    xres_v = x.rearrange("b (h p q) c -> (b h) p (q c)", p=P, q=Q)
    out_v = out.rearrange("b (h p q) c -> (b h) p (q c)", p=P, q=Q)
    x_v = x.rearrange("b (p k) c -> b p (k c)", k=K)

    with ExitStack() as ctx:
        def sb(name, shape, dt):
            return ctx.enter_context(nc.sbuf_tensor(name, shape, dt))

        def psum(name, shape, dt):
            return ctx.enter_context(nc.psum_tensor(name, shape, dt))

        def sem(name):
            return ctx.enter_context(nc.semaphore(name))

        ones = sb("ones", [P, P], BF16)
        eye = sb("eye", [P, P], BF16)
        eye32 = sb("eye32", [P, P], F32)
        upto = sb("upto", [P, P], BF16)
        before = sb("before", [P, P], BF16)
        rank_w = sb("rank_w", [P, P], BF16)
        minus_w = sb("minus_w", [P, P], BF16)
        numbers = sb("numbers", [P, 32], F32)
        numbers_i = sb("numbers_i", [P, 32], I32)
        bias_cut = sb("bias_cut", [P, 1], F32)
        bias_big = sb("bias_big", [P, 1], F32)
        bias_eps = sb("bias_eps", [P, 1], F32)
        one_row = sb("one_row", [1, P], F32)
        bias_row = sb("bias_row", [1, C], F32)
        w_in = sb("w_in", [P, 2, C], F32)
        w_scaled = sb("w_scaled", [P, 2, C], F32)
        adj_in = sb("adj_in", [P, 2, Q * N], I32)
        mask = sb("mask", [P, Q, N], BF16)
        mask_t = sb("mask_t", [P, K, ROWS], BF16)
        prefix = sb("prefix", [P, K, ROWS], BF16)
        past = sb("past", [P, K, ROWS], BF16)
        rank = sb("rank", [P, 2, K, ROWS], BF16)
        late = sb("late", [P, K, ROWS], BF16)
        late_sum = sb("late_sum", [P, K + 1, ROWS], BF16)
        late_rank = sb("late_rank", [P, 2, K, ROWS], BF16)
        late_most = sb("late_most", [P, 1], F32)
        late_rounds = sb("late_rounds", [P, 2], I32)
        hot = sb("hot", [P, 2, K, ROWS], F16)
        late_hot = sb("late_hot", [P, K, ROWS], F16)
        x_in = sb("x_in", [P, K, C], F32)
        stats = sb("stats", [P, K, 6], F32)
        moments = sb("moments", [P, K, 2], F32)
        held = sb("held", [P, 4], F32)
        spread = sb("spread", [P, K], F32)
        gain = sb("gain", [P, K], F32)
        normed = sb("normed", [P, K, C], F32)
        h32 = sb("h32", [P, K, C], F32)
        h_hi = sb("h_hi", [P, 2, K, C], F16)
        h_lo = sb("h_lo", [P, 2, K, C], F16)
        h_t = sb("h_t", [P, 2, N], F32)
        best = sb("best", [P, 2, 2, ROWS], F32)
        fold = sb("fold", [P, 2, ROWS], F32)
        agg_t = sb("agg_t", [P, ROWS], F32)
        xres = sb("xres", [P, 2, Q * C], F32)
        result = sb("result", [P, 2, Q * C], F32)

        picked = [psum(f"picked{s}", [P, 2, ROWS], F32) for s in range(2)]
        ring = [psum(f"ring{s}", [P, ROWS], F32) for s in range(2)]
        ring16 = [r[:, :].bitcast(BF16).rearrange("p (k r) -> p k r", k=2) for r in ring]
        side = psum("side", [P, ROWS], F32)
        final = psum("final", [P, ROWS], F32)

        adj_loaded = [sem(f"adj_loaded{s}") for s in range(2)]
        xres_loaded = [sem(f"xres_loaded{s}") for s in range(2)]
        stored = [sem(f"stored{s}") for s in range(2)]
        x_loaded = sem("x_loaded")
        weights_loaded = sem("weights_loaded")
        basics_made = sem("basics_made")
        consts_made = sem("consts_made")
        mask_made = sem("mask_made")
        mask_turned = sem("mask_turned")
        ring_written = sem("ring_written")
        ring_read = sem("ring_read")
        prefix_step = sem("prefix_step")
        late_made = sem("late_made")
        late_step = sem("late_step")
        late_zeroed = sem("late_zeroed")
        side_written = sem("side_written")
        side_read = sem("side_read")
        late_reduced = sem("late_reduced")
        rounds_known = sem("rounds_known")
        hot_made = sem("hot_made")
        picked_written = sem("picked_written")
        picked_read = sem("picked_read")
        late_hot_made = [sem(f"late_hot_made{s}") for s in range(2)]
        late_written = [sem(f"late_written{s}") for s in range(2)]
        late_read = [sem(f"late_read{s}") for s in range(2)]
        fold_step = sem("fold_step")
        agg_made = sem("agg_made")
        final_written = sem("final_written")
        result_made = sem("result_made")
        stats_made = sem("stats_made")
        moments_made = sem("moments_made")
        spread_made = sem("spread_made")
        gain_made = sem("gain_made")
        normed_made = sem("normed_made")
        h_made = sem("h_made")
        lo_made = sem("lo_made")
        h_turned = sem("h_turned")

        block = ctx.enter_context(nc.Block())

        def over_groups(eng, step):
            with eng.Fori(0, ITERS - 1) as it:
                for u in range(UNROLL):
                    step(it, u)
            for u in range(UNROLL):
                step(ITERS - 1, u)

        def g_of(it, u):
            return it * UNROLL + u

        def at_end(it, u, ahead):
            return isinstance(it, int) and it * UNROLL + u + ahead >= GROUPS

        def side_index(batch, n):
            return 4 * batch + n + 1

        def side_count(g, parity):
            return (g - parity) * 2 + 3 + parity

        @block.sync
        def _(sp):
            def load_adj(g, slot):
                sp.dma_start(adj_in[:, slot, :], adj_v[g]).then_inc(adj_loaded[slot], 16)

            def load_xres(g, slot):
                sp.dma_start(xres[:, slot, :], xres_v[g]).then_inc(xres_loaded[slot], 16)

            load_adj(0, 0)
            sp.dma_start(x_in[:, :, :].rearrange("p k c -> p (k c)"), x_v[0]).then_inc(x_loaded, 16)
            load_adj(1, 1)
            sp.dma_start(w_in[:, :, :], W.rearrange("(s p) n -> p s n", p=P)).then_inc(weights_loaded, 16)
            sp.dma_start(bias_row[:, :], b.rearrange("(a n) -> a n", a=1)).then_inc(weights_loaded, 16)
            load_xres(0, 0)
            for g in (0, 1):
                sp.wait_ge(mask_made, g + 1)
                load_adj(g + 2, g)

            def step(it, u):
                g = g_of(it, u)
                if not at_end(it, u, 1):
                    sp.wait_ge(result_made, g + 1)
                    load_xres(g + 1, (u + 1) % 2)
                if u % PER_BATCH == 0 and not at_end(it, u, PER_BATCH):
                    batch = it * (UNROLL // PER_BATCH) + u // PER_BATCH
                    sp.wait_ge(normed_made, batch + 1)
                    sp.dma_start(x_in[:, :, :].rearrange("p k c -> p (k c)"), x_v[batch + 1]).then_inc(x_loaded, 16)
                sp.wait_ge(result_made, g + 2)
                sp.dma_start(out_v[g], result[:, u % 2, :]).then_inc(stored[u % 2], 16)
                sp.wait_ge(stored[u % 2], 16 * (it * (UNROLL // 2) + u // 2 + 1))
                if not at_end(it, u, 4):
                    load_adj(g + 4, u % 2)

            over_groups(sp, step)

        @block.gpsimd
        def _(pool):
            nc.gpsimd.memset(ones[:, :], 1.0).then_inc(basics_made, 1)
            nc.gpsimd.memset(eye32[:, :], 1.0).then_inc(basics_made, 1)
            nc.gpsimd.iota(numbers_i[:, :], pattern=[[1, 32]], base=0, channel_multiplier=0).then_inc(basics_made, 1)
            nc.gpsimd.memset(one_row[:, :], 1.0).then_inc(basics_made, 1)
            nc.gpsimd.memset(bias_cut[:, :], -float(NEIGHBOURS)).then_inc(basics_made, 1)
            nc.gpsimd.memset(bias_big[:, :], -BIG).then_inc(basics_made, 1)
            nc.gpsimd.memset(bias_eps[:, :], EPS).then_inc(basics_made, 1)
            pool.wait_ge(basics_made, 7)
            line = dict(pattern=[[1, P]], channel_multiplier=-1, fill=0.0)
            nc.gpsimd.affine_select(out=upto[:, :], in_=ones[:, :], compare_op=ALU.is_ge, base=0, **line).then_inc(basics_made, 1)
            nc.gpsimd.affine_select(out=before[:, :], in_=ones[:, :], compare_op=ALU.is_gt, base=0, **line).then_inc(basics_made, 1)
            nc.gpsimd.affine_select(out=eye[:, :], in_=ones[:, :], compare_op=ALU.is_equal, base=0, **line).then_inc(basics_made, 1)
            nc.gpsimd.affine_select(out=eye32[:, :], in_=eye32[:, :], compare_op=ALU.is_equal, base=0, **line).then_inc(basics_made, 1)

            def class_sums(g):
                for k in range(1, K):
                    if k == 1 or k % 2 == 0:
                        pool.wait_ge(ring_read, g * RING + k // 2 + 1)
                    if k > 1:
                        pool.wait_ge(prefix_step, g * (K - 1) + k - 1)
                    first = mask_t[:, 0, :] if k == 1 else prefix[:, k - 1, :]
                    nc.gpsimd.tensor_tensor(prefix[:, k, :], first, mask_t[:, k, :], ALU.add).then_inc(prefix_step, 1)

            def late_sums(g):
                pool.wait_ge(late_made, g + 1)
                for k in range(2, K + 1):
                    if k > 2:
                        pool.wait_ge(late_step, g * (K - 1) + k - 2)
                    first = late[:, 0, :] if k == 2 else late_sum[:, k - 1, :]
                    nc.gpsimd.tensor_tensor(late_sum[:, k, :], first, late[:, k - 1, :], ALU.add).then_inc(late_step, 1)

            def low_part(batch, slot):
                pool.wait_ge(h_made, 2 * batch + 2)
                nc.gpsimd.tensor_tensor(h_lo[:, slot, :, :], h32[:, :, :], h_hi[:, slot, :, :], ALU.subtract).then_inc(lo_made, 1)

            class_sums(0)
            low_part(0, 0)
            late_sums(0)

            def step(it, u):
                if at_end(it, u, 1):
                    return
                class_sums(g_of(it, u) + 1)
                if u % PER_BATCH == PER_BATCH - 1:
                    batch = it * (UNROLL // PER_BATCH) + (u + 1) // PER_BATCH
                    low_part(batch, ((u + 1) // PER_BATCH) % 2)
                late_sums(g_of(it, u) + 1)

            over_groups(pool, step)

        @block.scalar
        def _(act):
            act.wait_ge(basics_made, 11)

            def turned_mask(g):
                for n in range(T_USES):
                    act.wait_ge(ring_written, g * RING + n + 1)
                    nc.scalar.copy(mask_t[:, 2 * n:2 * n + 2, :], ring16[n % 2]).then_inc(ring_read, 1)

            def stage(g, first, dst, bias):
                for k in range(K):
                    n = first + k
                    act.wait_ge(ring_written, g * RING + n + 1)
                    nc.scalar.activation(dst[:, k, :], ring[n % 2][:, :], ACT.Relu, bias=bias[:, 0:1]).then_inc(ring_read, 1)

            def spreads(batch):
                act.wait_ge(moments_made, K * batch + K)
                nc.scalar.activation(spread[:, :], moments[:, :, 1], ACT.Sqrt, bias=bias_eps[:, 0:1]).then_inc(spread_made, 1)

            def relu_parts(batch, slot):
                act.wait_ge(normed_made, batch + 1)
                nc.scalar.activation(h_hi[:, slot, :, :], normed[:, :, :], ACT.Relu).then_inc(h_made, 1)
                nc.scalar.activation(h32[:, :, :], normed[:, :, :], ACT.Relu).then_inc(h_made, 1)

            def turned_h(batch, slot):
                dst = h_t[:, slot, :].rearrange("c (a k) -> c k a", k=K)
                for n in range(2):
                    act.wait_ge(side_written, side_index(batch, n))
                    nc.scalar.copy(dst[:, 4 * n:4 * n + 4, :], side[:, :].rearrange("c (k a) -> c k a", k=4)).then_inc(h_turned, 1)

            spreads(0)
            turned_mask(0)
            relu_parts(0, 0)
            stage(0, T_USES, past, bias_cut)
            stage(0, T_USES + K, rank[:, 0], bias_big)
            turned_h(0, 0)
            stage(0, T_USES + 2 * K, late_rank[:, 0], bias_big)

            def step(it, u):
                if at_end(it, u, 1):
                    return
                g1, s1 = g_of(it, u) + 1, (u + 1) % 2
                new_batch = u % PER_BATCH == PER_BATCH - 1
                batch = it * (UNROLL // PER_BATCH) + (u + 1) // PER_BATCH
                slot = ((u + 1) // PER_BATCH) % 2
                turned_mask(g1)
                if new_batch:
                    spreads(batch)
                stage(g1, T_USES, past, bias_cut)
                stage(g1, T_USES + K, rank[:, s1], bias_big)
                if new_batch:
                    relu_parts(batch, slot)
                    turned_h(batch, slot)
                stage(g1, T_USES + 2 * K, late_rank[:, s1], bias_big)

            over_groups(act, step)

        @block.tensor
        def _(pe):
            def take(n, g):
                if isinstance(g, int) and g * RING + n < 2:
                    return
                pe.wait_ge(ring_read, g * RING + n - 1)

            def turn_mask(g, n):
                if n == 0:
                    pe.wait_ge(mask_made, g + 1)
                take(n, g)
                for j in range(2):
                    k = 2 * n + j
                    for q in range(Q):
                        last = nc.tensor.transpose(ring16[n % 2][:, j, q * P:(q + 1) * P], mask[:, q, k::K], eye[:, :])
                last.then_inc(ring_written, 1)

            def accumulate(n, g, terms):
                take(n, g)
                for i, (w, m) in enumerate(terms):
                    last = nc.tensor.matmul(ring[n % 2][:, :], w[:, :], m, start=(i == 0), stop=(i == len(terms) - 1))
                last.then_inc(ring_written, 1)

            def cutoff(g, k):
                if k == 0:
                    pe.wait_ge(prefix_step, (g + 1) * (K - 1))
                own = mask_t[:, 0, :] if k == 0 else prefix[:, k, :]
                accumulate(T_USES + k, g, [(before, prefix[:, K - 1, :]), (eye, own)])

            def ranks(g, k):
                n = T_USES + K + k
                pe.wait_ge(ring_read, g * RING + T_USES + k + 1)
                accumulate(n, g, [(rank_w, mask_t[:, k, :]), (minus_w, past[:, k, :])])

            def late_ranks(g, k):
                if k == 0:
                    pe.wait_ge(late_step, (g + 1) * (K - 1))
                terms = [(rank_w, late[:, k, :])]
                if k:
                    terms.append((ones, late[:, 0, :] if k == 1 else late_sum[:, k, :]))
                accumulate(T_USES + 2 * K + k, g, terms)

            def count(g, parity):
                if parity == 0:
                    pe.wait_ge(h_turned, g + 2)
                else:
                    pe.wait_ge(rounds_known, g)
                nc.tensor.matmul(side[:, :], ones[:, :], late_sum[:, K, :], start=True, stop=True).then_inc(side_written, 1)

            def turn_h(batch, it_first):
                pe.wait_ge(h_made, 2 * batch + 2)
                for n in range(2):
                    if n:
                        pe.wait_ge(h_turned, 2 * batch + 1)
                    elif not it_first:
                        pe.wait_ge(rounds_known, 2 * batch)
                    for j in range(4):
                        last = nc.tensor.transpose(side[:, j * P:(j + 1) * P], h32[:, 4 * n + j, :], eye32[:, :])
                    last.then_inc(side_written, 1)

            def pick(dst, k, onehot, slot, start, stop):
                nc.tensor.matmul(dst, h_hi[:, slot, k, :], onehot, start=start, stop=False)
                return nc.tensor.matmul(dst, h_lo[:, slot, k, :], onehot, start=False, stop=stop)

            rounds_done = pe.alloc_register("pe_rounds_done")
            pe.reg_mov(rounds_done, 0)

            pe.wait_ge(basics_made, 11)
            pe.wait_ge(consts_made, 4)
            for n in range(T_USES):
                turn_mask(0, n)
            for k in range(K):
                cutoff(0, k)
            for k in range(K):
                ranks(0, k)
            turn_h(0, True)
            for k in range(K):
                late_ranks(0, k)
            count(0, 0)

            def step(it, u):
                g = g_of(it, u)
                more = not at_end(it, u, 1)
                g1 = g + 1
                slot = (u // PER_BATCH) % 2
                new_batch = u % PER_BATCH == PER_BATCH - 1
                done = pe.snap(rounds_done)
                pe.wait_ge(late_read[0], done + 1)
                pe.wait_ge(late_read[1], done + 1)
                if u % PER_BATCH == 0:
                    batch = it * (UNROLL // PER_BATCH) + u // PER_BATCH
                    pe.wait_ge(lo_made, batch + 1)
                for t in range(BASE):
                    pe.wait_ge(hot_made, g * BASE + t + 1)
                    for p in range(PAIRS):
                        use = t * PAIRS + p
                        if use >= 2:
                            pe.wait_ge(picked_read, g * (BASE * PAIRS) + use - 1)
                        for j in range(2):
                            last = pick(picked[p % 2][:, j, :], 2 * p + j, hot[:, t % 2, 2 * p + j, :], slot, True, True)
                        last.then_inc(picked_written, 1)
                        if more and t == 0:
                            turn_mask(g1, p)
                        if more and t == BASE - 2:
                            cutoff(g1, 2 * p)
                            cutoff(g1, 2 * p + 1)
                        if more and t == BASE - 1:
                            ranks(g1, 2 * p)
                            ranks(g1, 2 * p + 1)
                if more and new_batch:
                    turn_h(it * (UNROLL // PER_BATCH) + (u + 1) // PER_BATCH, False)
                pe.wait_ge(rounds_known, 1)
                pe.wait_ge(rounds_known, g + 1)
                n = pe.value_load(late_rounds[0:1, u % 2:u % 2 + 1], min_val=1, max_val=NEIGHBOURS)
                with pe.Fori(0, n) as r:
                    pe.wait_ge(picked_read, (g + 1) * (BASE * PAIRS))
                    for s in range(2):
                        pe.wait_ge(late_hot_made[s], done + (r + (g + 1)))
                        pe.wait_ge(late_read[s], done + r + 1)
                        for k in range(s * HALF, (s + 1) * HALF):
                            last = pick(picked[s][:, 0, :], k, late_hot[:, k, :], slot, k == s * HALF, k == (s + 1) * HALF - 1)
                        last.then_inc(late_written[s], 1)
                pe.reg_add(rounds_done, rounds_done, n)
                if more:
                    for k in range(K):
                        late_ranks(g1, k)
                    count(g1, (u + 1) % 2)
                pe.wait_ge(agg_made, g + 1)
                pe.wait_ge(result_made, g + 1)
                if u % PER_BATCH == 0:
                    pe.wait_ge(h_turned, 2 * (it * (UNROLL // PER_BATCH) + u // PER_BATCH) + 2)
                first = (u % PER_BATCH) * ROWS
                for q in range(Q):
                    dst = final[:, q * C:(q + 1) * C]
                    nc.tensor.matmul(dst, h_t[:, slot, first + q:first + ROWS:Q], w_scaled[:, 0, :], start=True, stop=False)
                    nc.tensor.matmul(dst, agg_t[:, q * P:(q + 1) * P], w_scaled[:, 1, :], start=False, stop=False)
                    last = nc.tensor.matmul(dst, one_row[:, :], bias_row[:, :], start=False, stop=True)
                last.then_inc(final_written, 1)

            over_groups(pe, step)

        @block.vector
        def _(dve):
            def make_mask(it, u, g, slot, uses):
                dve.wait_ge(adj_loaded[slot], uses)
                if not (isinstance(g, int) and g == 0):
                    dve.wait_ge(ring_written, (g - 1) * RING + T_USES)
                nc.vector.tensor_scalar(mask[:, :, :].rearrange("p q n -> p (q n)"), adj_in[:, slot, :], 0.0, None,
                                        ALU.not_equal).then_inc(mask_made, 1)

            def moments_of(batch):
                dve.wait_ge(x_loaded, 16 * batch + 16)
                for k in range(K):
                    nc.vector.bn_stats(stats[:, k, :], x_in[:, k, :]).then_inc(stats_made, 1)
                dve.wait_ge(stats_made, K * (batch + 1))
                nc.vector.memset(held[:, 3:4], 0.0)
                for k in range(K):
                    nc.vector.bn_aggr(moments[:, k, :], stats[:, k, :]).then_inc(moments_made, 1)

            def normalize(batch):
                dve.wait_ge(spread_made, batch + 1)
                nc.vector.reciprocal(gain[:, :], spread[:, :]).then_inc(gain_made, 1)
                dve.wait_ge(gain_made, 2 * batch + 1)
                nc.vector.tensor_scalar(gain[:, :], gain[:, :], SCALE, None, ALU.mult).then_inc(gain_made, 1)
                dve.wait_ge(gain_made, 2 * batch + 2)
                for k in range(K):
                    last = nc.vector.tensor_scalar(normed[:, k, :], x_in[:, k, :], moments[:, k, 0:1], gain[:, k:k + 1],
                                                   ALU.subtract, ALU.mult)
                last.then_inc(normed_made, 1)

            def make_hot(t, s):
                nc.vector.tensor_scalar(hot[:, (t - 1) % 2, :, :], rank[:, s, :, :], float(t), None,
                                        ALU.is_equal).then_inc(hot_made, 1)

            def find_late(g, s):
                dve.wait_ge(ring_read, g * RING + T_USES + 2 * K)
                nc.vector.tensor_scalar(late[:, :, :], rank[:, s, :, :], float(BASE), None, ALU.is_gt).then_inc(late_made, 1)

            def count_rounds(g, s):
                dve.wait_ge(side_written, side_count(g, s))
                nc.vector.tensor_reduce(late_most[:, :], side[:, :], AX.X, ALU.max).then_inc(late_reduced, 1)
                dve.wait_ge(late_reduced, g + 1)
                nc.vector.tensor_scalar(late_rounds[:, s:s + 1], late_most[:, :], 1.0, None, ALU.max).then_inc(rounds_known, 1)

            rounds_done = dve.alloc_register("dve_rounds_done")
            dve.reg_mov(rounds_done, 0)
            for i, opened in enumerate((result_made, late_read[0], late_read[1])):
                nc.vector.memset(held[:, i:i + 1], 0.0).then_inc(opened, 1)
            dve.wait_ge(basics_made, 11)
            nc.vector.tensor_copy(numbers[:, :], numbers_i[:, :]).then_inc(consts_made, 1)
            nc.vector.scalar_tensor_tensor(out=rank_w[:, :], in0=eye[:, :], scalar=BIG, in1=upto[:, :], op0=ALU.mult,
                                           op1=ALU.add).then_inc(consts_made, 1)
            nc.vector.tensor_scalar(minus_w[:, :], eye[:, :], -BIG, None, ALU.mult).then_inc(consts_made, 1)
            dve.wait_ge(weights_loaded, 32)
            nc.vector.tensor_scalar(w_scaled[:, :, :], w_in[:, :, :], 1.0 / SCALE, None, ALU.mult).then_inc(consts_made, 1)
            make_mask(0, 0, 0, 0, 16)
            moments_of(0)
            normalize(0)
            make_mask(0, 0, 1, 1, 16)
            find_late(0, 0)
            make_hot(1, 0)
            count_rounds(0, 0)
            dve.wait_ge(consts_made, 4)

            def step(it, u):
                g, s = g_of(it, u), u % 2
                more = not at_end(it, u, 1)
                new_batch = more and u % PER_BATCH == PER_BATCH - 1
                batch = it * (UNROLL // PER_BATCH) + (u + 1) // PER_BATCH

                def keep_max(t):
                    for p in range(PAIRS):
                        use = (t - 1) * PAIRS + p
                        dve.wait_ge(picked_written, g * (BASE * PAIRS) + use + 1)
                        if use < 2:
                            nc.vector.tensor_scalar(best[:, p % 2, :, :], picked[p % 2][:, :, :], 0.0, None,
                                                    ALU.max).then_inc(picked_read, 1)
                        else:
                            nc.vector.tensor_tensor(best[:, p % 2, :, :], picked[p % 2][:, :, :], best[:, p % 2, :, :],
                                                    ALU.max).then_inc(picked_read, 1)

                for t in range(1, BASE + 1):
                    if t < BASE:
                        make_hot(t + 1, s)
                    keep_max(t)
                    if t == 1 and new_batch:
                        moments_of(batch)
                    if t == 2 and not at_end(it, u, 2):
                        make_mask(it, u, g + 2, s, 16 * (it * (UNROLL // 2) + u // 2 + 2))
                    if t == 3 and new_batch:
                        normalize(batch)
                if more:
                    find_late(g + 1, 1 - s)

                done = dve.snap(rounds_done)
                dve.wait_ge(rounds_known, 1)
                dve.wait_ge(rounds_known, g + 1)
                n = dve.value_load(late_rounds[0:1, s:s + 1], min_val=1, max_val=NEIGHBOURS)
                dve.wait_ge(ring_read, (g + 1) * RING)

                def make_late_hot(i, which):
                    part = slice(i * HALF, (i + 1) * HALF)
                    nc.vector.tensor_scalar(late_hot[:, part, :], late_rank[:, s, part, :], which, None,
                                            ALU.is_equal).then_inc(late_hot_made[i], 1)

                for i in range(2):
                    make_late_hot(i, numbers[:, 1:2])
                with dve.Fori(0, n) as r:
                    for i in range(2):
                        dve.wait_ge(late_written[i], done + r + 1)
                        nc.vector.tensor_tensor(best[:, i, 0, :], picked[i][:, 0, :], best[:, i, 0, :],
                                                ALU.max).then_inc(late_read[i], 1)
                        make_late_hot(i, numbers[:, bass.ds(r + 2, 1)])
                dve.reg_add(rounds_done, rounds_done, n)
                done = dve.snap(rounds_done)
                if more:
                    make_hot(1, 1 - s)
                for i in range(2):
                    dve.wait_ge(late_read[i], done + 1)
                nc.vector.tensor_tensor(fold[:, :, :], best[:, 0, :, :], best[:, 1, :, :], ALU.max).then_inc(fold_step, 1)
                dve.wait_ge(fold_step, g + 1)
                nc.vector.tensor_tensor(agg_t[:, :], fold[:, 0, :], fold[:, 1, :], ALU.max).then_inc(agg_made, 1)
                if more:
                    count_rounds(g + 1, 1 - s)
                dve.wait_ge(final_written, g + 1)
                dve.wait_ge(xres_loaded[s], 16 * (it * (UNROLL // 2) + u // 2 + 1))
                nc.vector.scalar_tensor_tensor(out=result[:, s, :], in0=final[:, :], scalar=0.0, in1=xres[:, s, :],
                                               op0=ALU.max, op1=ALU.add).then_inc(result_made, 1)

            over_groups(dve, step)


_INS = ["x", "adj", "L0_gnn_W", "L0_gnn_b"]


def kernel(**inputs):
    import numpy as _np
    import concourse.bacc as _bacc
    from concourse import mybir as _mybir
    from concourse.bass_utils import run_bass_kernel_spmd as _run

    nc = _bacc.Bacc("TRN2", target_bir_lowering=False, num_devices=1)
    arrays, args = {}, []
    for name in _INS:
        a = _np.ascontiguousarray(inputs[name])
        arrays[f"in_{name}_dram"] = a
        args.append(nc.dram_tensor(f"in_{name}_dram", a.shape, _mybir.dt.from_np(a.dtype), kind="ExternalInput").ap())
    shape = inputs["x"].shape
    args.append(nc.dram_tensor("out_0_dram", shape, _mybir.dt.float32, kind="ExternalOutput").ap())
    build(nc, *args)
    r = _run(nc, [arrays], core_ids=[0])
    return r.results[0]["out_0_dram"]
```

```python
from contextlib import ExitStack

import concourse.bass as bass
from concourse import mybir

F32 = mybir.dt.float32
F16 = mybir.dt.float16
BF16 = mybir.dt.bfloat16
I32 = mybir.dt.int32
ALU = mybir.AluOpType
ACT = mybir.ActivationFunctionType
AX = mybir.AxisListType

P = 128
NEIGHBOURS = 25
BASE = 5
EPS = 1e-5
SCALE = 4096.0
BIG = 128.0


def build(nc, x, adj, W, b, out):
    B, N, C = x.shape
    K = N // P
    ROWS = 512
    Q = ROWS // P
    GROUPS = B * N // ROWS
    PER_BATCH = N // ROWS
    UNROLL = 2 * PER_BATCH
    ITERS = GROUPS // UNROLL
    PAIRS = K // 2
    HALF = K // 2
    USES = BASE * PAIRS
    READ = USES - 2
    LATE_USE, CUT_USE, RANK_USE = 4, 9, 13
    COUNT_USE, MOMENTS_USE, SPREAD_USE, NORMAL_USE, RELU_USE = LATE_USE + 5, 5, 8, 10, 13
    TURNS = K // 2
    FIRST_RING = 2 * TURNS + 2 * K
    RING = 3 * K + TURNS
    LATE_AT, CUT_AT, RANK_AT, TURN_AT = 0, K, 2 * K, 3 * K
    assert C == P and K == 8 and PER_BATCH == 2 and BASE >= 5
    assert RING % 2 == 0 and FIRST_RING % 2 == 0

    adj_v = adj.rearrange("b (h p q) j -> (b h) p (q j)", p=P, q=Q)
    xres_v = x.rearrange("b (h p q) c -> (b h) p (q c)", p=P, q=Q)
    out_v = out.rearrange("b (h p q) c -> (b h) p (q c)", p=P, q=Q)
    x_v = x.rearrange("b (p k) c -> b p (k c)", k=K)

    with ExitStack() as ctx:
        def sb(name, shape, dt):
            return ctx.enter_context(nc.sbuf_tensor(name, shape, dt))

        def psum(name, shape, dt):
            return ctx.enter_context(nc.psum_tensor(name, shape, dt))

        def sem(name):
            return ctx.enter_context(nc.semaphore(name))

        ones = sb("ones", [P, P], BF16)
        eye = sb("eye", [P, P], BF16)
        eye32 = sb("eye32", [P, P], F32)
        upto = sb("upto", [P, P], BF16)
        before = sb("before", [P, P], BF16)
        rank_w = sb("rank_w", [P, P], BF16)
        minus_w = sb("minus_w", [P, P], BF16)
        numbers = sb("numbers", [P, 32], F32)
        numbers_i = sb("numbers_i", [P, 32], I32)
        bias_cut = sb("bias_cut", [P, 1], F32)
        bias_big = sb("bias_big", [P, 1], F32)
        bias_eps = sb("bias_eps", [P, 1], F32)
        one_row = sb("one_row", [1, P], F32)
        bias_row = sb("bias_row", [1, C], F32)
        w_in = sb("w_in", [P, 2, C], F32)
        w_scaled = sb("w_scaled", [P, 2, C], F32)
        adj_in = sb("adj_in", [P, 2, Q * N], I32)
        mask = sb("mask", [P, Q, N], BF16)
        mask_t = sb("mask_t", [P, K, ROWS], BF16)
        prefix = sb("prefix", [P, K, ROWS], BF16)
        past = sb("past", [P, K, ROWS], BF16)
        rank = sb("rank", [P, 2, K, ROWS], BF16)
        late = sb("late", [P, K, ROWS], BF16)
        late_sum = sb("late_sum", [P, K + 1, ROWS], BF16)
        late_rank = sb("late_rank", [P, K, ROWS], BF16)
        late_most = sb("late_most", [P, 1], F32)
        late_rounds = sb("late_rounds", [P, 2], I32)
        hot = sb("hot", [P, 3, K, ROWS], F16)
        late_hot = sb("late_hot", [P, K, ROWS], F16)
        x_in = sb("x_in", [P, K, C], F32)
        stats = sb("stats", [P, K, 6], F32)
        moments = sb("moments", [P, K, 2], F32)
        held = sb("held", [P, 4], F32)
        spread = sb("spread", [P, K], F32)
        gain = sb("gain", [P, K], F32)
        h32 = sb("h32", [P, K, C], F32)
        h_hi = sb("h_hi", [P, 2, K, C], F16)
        h_lo = sb("h_lo", [P, 2, K, C], F16)
        h_t = sb("h_t", [P, 2, N], F32)
        best = sb("best", [P, 2, 2, ROWS], F32)
        fold = sb("fold", [P, 2, ROWS], F32)
        agg_t = sb("agg_t", [P, ROWS], F32)
        xres = sb("xres", [P, 2, Q * C], F32)
        result = sb("result", [P, 2, Q * C], F32)

        picked = [psum(f"picked{s}", [P, 2, ROWS], F32) for s in range(2)]
        ring = [psum(f"ring{s}", [P, ROWS], F32) for s in range(2)]
        ring16 = [r[:, :].bitcast(BF16).rearrange("p (k r) -> p k r", k=2) for r in ring]
        side = psum("side", [P, ROWS], F32)
        final = psum("final", [P, ROWS], F32)

        adj_loaded = [sem(f"adj_loaded{s}") for s in range(2)]
        xres_loaded = [sem(f"xres_loaded{s}") for s in range(2)]
        stored = [sem(f"stored{s}") for s in range(2)]
        x_loaded = sem("x_loaded")
        weights_loaded = sem("weights_loaded")
        basics_made = sem("basics_made")
        consts_made = sem("consts_made")
        mask_made = sem("mask_made")
        ring_written = sem("ring_written")
        ring_read = sem("ring_read")
        prefix_step = sem("prefix_step")
        late_made = sem("late_made")
        late_step = sem("late_step")
        count_written = sem("count_written")
        late_reduced = sem("late_reduced")
        rounds_known = sem("rounds_known")
        hot_made = sem("hot_made")
        picked_written = sem("picked_written")
        picked_copied = sem("picked_copied")
        picked_read = sem("picked_read")
        late_hot_made = [sem(f"late_hot_made{s}") for s in range(2)]
        late_written = [sem(f"late_written{s}") for s in range(2)]
        late_read = [sem(f"late_read{s}") for s in range(2)]
        fold_step = sem("fold_step")
        agg_made = sem("agg_made")
        final_written = sem("final_written")
        result_made = sem("result_made")
        stats_made = sem("stats_made")
        moments_made = sem("moments_made")
        spread_made = sem("spread_made")
        gain_made = sem("gain_made")
        normed_made = sem("normed_made")
        h_made = sem("h_made")
        lo_made = sem("lo_made")
        h_written = sem("h_written")
        h_turned = sem("h_turned")

        block = ctx.enter_context(nc.Block())

        def over_groups(eng, step):
            with eng.Fori(0, ITERS - 1) as it:
                for u in range(UNROLL):
                    step(it, u)
            for u in range(UNROLL):
                step(ITERS - 1, u)

        def g_of(it, u):
            return it * UNROLL + u

        def batch_of(it, u):
            return it * (UNROLL // PER_BATCH) + u // PER_BATCH

        def at_end(it, u, ahead):
            return isinstance(it, int) and it * UNROLL + u + ahead >= GROUPS

        def ring_of(it, u):
            skipped = TURNS if at_end(it, u, 1) else 0
            return (it * UNROLL + u) * RING + FIRST_RING - skipped

        @block.sync
        def _(sp):
            def load_adj(g, slot):
                sp.dma_start(adj_in[:, slot, :], adj_v[g]).then_inc(adj_loaded[slot], 16)

            def load_xres(g, slot):
                sp.dma_start(xres[:, slot, :], xres_v[g]).then_inc(xres_loaded[slot], 16)

            def load_x(batch):
                sp.dma_start(x_in[:, :, :].rearrange("p k c -> p (k c)"), x_v[batch]).then_inc(x_loaded, 16)

            load_adj(0, 0)
            load_x(0)
            load_adj(1, 1)
            sp.dma_start(w_in[:, :, :], W.rearrange("(s p) n -> p s n", p=P)).then_inc(weights_loaded, 16)
            sp.dma_start(bias_row[:, :], b.rearrange("(a n) -> a n", a=1)).then_inc(weights_loaded, 16)
            load_xres(0, 0)
            for g in (0, 1):
                sp.wait_ge(mask_made, g + 1)
                load_adj(g + 2, g)

            def step(it, u):
                g = g_of(it, u)
                if not at_end(it, u, 1):
                    sp.wait_ge(result_made, g + 1)
                    load_xres(g + 1, (u + 1) % 2)
                if u % PER_BATCH == 0 and not at_end(it, u, PER_BATCH):
                    sp.wait_ge(normed_made, batch_of(it, u) + 1)
                    load_x(batch_of(it, u) + 1)
                sp.wait_ge(result_made, g + 2)
                sp.dma_start(out_v[g], result[:, u % 2, :]).then_inc(stored[u % 2], 16)
                sp.wait_ge(stored[u % 2], 16 * (it * (UNROLL // 2) + u // 2 + 1))
                if not at_end(it, u, 4):
                    load_adj(g + 4, u % 2)

            over_groups(sp, step)

        @block.gpsimd
        def _(pool):
            nc.gpsimd.memset(ones[:, :], 1.0).then_inc(basics_made, 1)
            nc.gpsimd.memset(eye32[:, :], 1.0).then_inc(basics_made, 1)
            nc.gpsimd.iota(numbers_i[:, :], pattern=[[1, 32]], base=0, channel_multiplier=0).then_inc(basics_made, 1)
            nc.gpsimd.memset(one_row[:, :], 1.0).then_inc(basics_made, 1)
            nc.gpsimd.memset(bias_cut[:, :], -float(NEIGHBOURS)).then_inc(basics_made, 1)
            nc.gpsimd.memset(bias_big[:, :], -BIG).then_inc(basics_made, 1)
            nc.gpsimd.memset(bias_eps[:, :], EPS).then_inc(basics_made, 1)
            pool.wait_ge(basics_made, 7)
            line = dict(pattern=[[1, P]], channel_multiplier=-1, fill=0.0)
            nc.gpsimd.affine_select(out=eye[:, :], in_=ones[:, :], compare_op=ALU.is_equal, base=0, **line).then_inc(basics_made, 1)
            nc.gpsimd.affine_select(out=upto[:, :], in_=ones[:, :], compare_op=ALU.is_ge, base=0, **line).then_inc(basics_made, 1)
            nc.gpsimd.affine_select(out=before[:, :], in_=ones[:, :], compare_op=ALU.is_gt, base=0, **line).then_inc(basics_made, 1)
            nc.gpsimd.affine_select(out=eye32[:, :], in_=eye32[:, :], compare_op=ALU.is_equal, base=0, **line).then_inc(basics_made, 1)

            def class_sums(g, turned):
                for k in range(1, K):
                    if k == 1 or k % 2 == 0:
                        pool.wait_ge(ring_read, turned + k // 2 + 1)
                    if k > 1:
                        pool.wait_ge(prefix_step, g * (K - 1) + k - 1)
                    first = mask_t[:, 0, :] if k == 1 else prefix[:, k - 1, :]
                    nc.gpsimd.tensor_tensor(prefix[:, k, :], first, mask_t[:, k, :], ALU.add).then_inc(prefix_step, 1)

            def late_sums(g):
                pool.wait_ge(late_made, g + 1)
                for k in range(2, K + 1):
                    if k > 2:
                        pool.wait_ge(late_step, g * (K - 1) + k - 2)
                    first = late[:, 0, :] if k == 2 else late_sum[:, k - 1, :]
                    nc.gpsimd.tensor_tensor(late_sum[:, k, :], first, late[:, k - 1, :], ALU.add).then_inc(late_step, 1)

            def low_part(batch, slot):
                pool.wait_ge(h_made, 2 * batch + 2)
                nc.gpsimd.tensor_tensor(h_lo[:, slot, :, :], h32[:, :, :], h_hi[:, slot, :, :], ALU.subtract).then_inc(lo_made, 1)

            class_sums(0, 0)
            low_part(0, 0)
            late_sums(0)
            class_sums(1, FIRST_RING - TURNS)

            def step(it, u):
                g = g_of(it, u)
                if not at_end(it, u, 1):
                    if u % PER_BATCH == PER_BATCH - 1:
                        low_part(batch_of(it, u + 1), ((u + 1) // PER_BATCH) % 2)
                    late_sums(g + 1)
                if not at_end(it, u, 2):
                    class_sums(g + 2, ring_of(it, u) + TURN_AT)

            over_groups(pool, step)

        @block.scalar
        def _(act):
            act.wait_ge(basics_made, 8)

            def turned_mask(at, n):
                act.wait_ge(ring_written, at + n + 1)
                nc.scalar.copy(mask_t[:, 2 * n:2 * n + 2, :], ring16[n % 2]).then_inc(ring_read, 1)

            def stage(at, k, dst, bias):
                act.wait_ge(ring_written, at + k + 1)
                nc.scalar.activation(dst[:, k, :], ring[k % 2][:, :], ACT.Relu, bias=bias[:, 0:1]).then_inc(ring_read, 1)

            def spreads(batch):
                act.wait_ge(moments_made, K * batch + K)
                nc.scalar.activation(spread[:, :], moments[:, :, 1], ACT.Sqrt, bias=bias_eps[:, 0:1]).then_inc(spread_made, 1)

            def relu_parts(batch, slot):
                act.wait_ge(normed_made, batch + 1)
                nc.scalar.activation(h_hi[:, slot, :, :], h32[:, :, :], ACT.Relu).then_inc(h_made, 1)
                act.wait_ge(h_made, 2 * batch + 1)
                nc.scalar.activation(h32[:, :, :], h32[:, :, :], ACT.Relu).then_inc(h_made, 1)

            def turned_h(batch, slot):
                dst = h_t[:, slot, :].rearrange("c (a k) -> c k a", k=K)
                for n, bank in enumerate((side, final)):
                    act.wait_ge(h_written, 2 * batch + n + 1)
                    nc.scalar.copy(dst[:, 4 * n:4 * n + 4, :], bank[:, :].rearrange("c (k a) -> c k a", k=4)).then_inc(h_turned, 1)

            def first_maxima(g, s, new_best):
                act.wait_ge(picked_written, g * USES + s + 1)
                if new_best:
                    act.wait_ge(fold_step, g)
                nc.scalar.copy(best[:, s, :, :], picked[s][:, :, :]).then_inc(picked_copied, 1)

            spreads(0)
            for n in range(TURNS):
                turned_mask(0, n)
            relu_parts(0, 0)
            for k in range(K):
                stage(TURNS, k, past, bias_cut)
            for k in range(K):
                stage(TURNS + K, k, rank[:, 0], bias_big)
            turned_h(0, 0)
            for s in range(2):
                first_maxima(0, s, False)
            for n in range(TURNS):
                turned_mask(FIRST_RING - TURNS, n)

            def step(it, u):
                g = g_of(it, u)
                at = ring_of(it, u)
                more = not at_end(it, u, 1)
                new_batch = more and u % PER_BATCH == PER_BATCH - 1
                batch, slot = batch_of(it, u + 1), ((u + 1) // PER_BATCH) % 2
                for use in range(PAIRS, USES):
                    for i in (0, 1):
                        if 0 <= use - LATE_USE < PAIRS:
                            stage(at + LATE_AT, 2 * (use - LATE_USE) + i, late_rank, bias_big)
                        if 0 <= use - CUT_USE < PAIRS and more:
                            stage(at + CUT_AT, 2 * (use - CUT_USE) + i, past, bias_cut)
                        if 0 <= use - RANK_USE < PAIRS and more:
                            stage(at + RANK_AT, 2 * (use - RANK_USE) + i, rank[:, (u + 1) % 2], bias_big)
                    if use == SPREAD_USE and new_batch:
                        spreads(batch)
                    if use == RELU_USE and new_batch:
                        relu_parts(batch, slot)
                if new_batch:
                    turned_h(batch, slot)
                if more:
                    for s in range(2):
                        first_maxima(g + 1, s, True)
                if not at_end(it, u, 2):
                    for k in range(TURNS):
                        turned_mask(at + TURN_AT, k)

            over_groups(act, step)

        @block.tensor
        def _(pe):
            def take(at):
                if not isinstance(at, int) or at >= 2:
                    pe.wait_ge(ring_read, at - 1)

            def turn_mask(g, at, n):
                if n == 0:
                    pe.wait_ge(mask_made, g + 1)
                take(at + n)
                for j in range(2):
                    for q in range(Q):
                        last = nc.tensor.transpose(ring16[n % 2][:, j, q * P:(q + 1) * P], mask[:, q, 2 * n + j::K], eye[:, :])
                last.then_inc(ring_written, 1)

            def accumulate(at, k, terms):
                take(at + k)
                for i, (w, m) in enumerate(terms):
                    last = nc.tensor.matmul(ring[k % 2][:, :], w[:, :], m, start=(i == 0), stop=(i == len(terms) - 1))
                last.then_inc(ring_written, 1)

            def cutoff(g, at, k):
                if k == 0:
                    pe.wait_ge(prefix_step, (g + 1) * (K - 1))
                own = mask_t[:, 0, :] if k == 0 else prefix[:, k, :]
                accumulate(at, k, [(before, prefix[:, K - 1, :]), (eye, own)])

            def ranks(at, cut_at, k):
                pe.wait_ge(ring_read, cut_at + k + 1)
                accumulate(at, k, [(rank_w, mask_t[:, k, :]), (minus_w, past[:, k, :])])

            def late_ranks(g, at, k):
                if k == 0:
                    pe.wait_ge(late_step, (g + 1) * (K - 1))
                terms = [(rank_w, late[:, k, :])]
                if k:
                    terms.append((ones, late[:, 0, :] if k == 1 else late_sum[:, k, :]))
                accumulate(at, k, terms)

            def count(g, parity):
                if parity == 0:
                    pe.wait_ge(h_turned, g + 2)
                else:
                    pe.wait_ge(rounds_known, g)
                nc.tensor.matmul(side[:, :], ones[:, :], late_sum[:, K, :], start=True, stop=True).then_inc(count_written, 1)

            def turn_h(batch, first):
                pe.wait_ge(h_made, 2 * batch + 2)
                for n, bank in enumerate((side, final)):
                    if not first:
                        pe.wait_ge((rounds_known, result_made)[n], 2 * batch)
                    for j in range(4):
                        last = nc.tensor.transpose(bank[:, j * P:(j + 1) * P], h32[:, 4 * n + j, :], eye32[:, :])
                    last.then_inc(h_written, 1)

            def pick(dst, k, onehot, slot, start, stop):
                nc.tensor.matmul(dst, h_hi[:, slot, k, :], onehot, start=start, stop=False)
                return nc.tensor.matmul(dst, h_lo[:, slot, k, :], onehot, start=False, stop=stop)

            def pick_pair(g, use, slot):
                t, p = use // PAIRS, use % PAIRS
                if p == 0:
                    pe.wait_ge(hot_made, g * BASE + t + 1)
                if use in (2, 3):
                    pe.wait_ge(picked_copied, g * 2 + use - 1)
                if use > 3:
                    pe.wait_ge(picked_read, g * READ + use - 3)
                for j in range(2):
                    last = pick(picked[p % 2][:, j, :], 2 * p + j, hot[:, t % 3, 2 * p + j, :], slot, True, True)
                last.then_inc(picked_written, 1)

            def project(g, it, u, new_batch):
                slot = (u // PER_BATCH) % 2
                pe.wait_ge(agg_made, g + 1)
                pe.wait_ge(result_made, g + 1)
                if u % PER_BATCH == 0:
                    pe.wait_ge(h_turned, 2 * batch_of(it, u) + 2)
                if new_batch:
                    pe.wait_ge(h_turned, 2 * batch_of(it, u + 1) + 2)
                first = (u % PER_BATCH) * ROWS
                for q in range(Q):
                    dst = final[:, q * C:(q + 1) * C]
                    nc.tensor.matmul(dst, h_t[:, slot, first + q:first + ROWS:Q], w_scaled[:, 0, :], start=True, stop=False)
                    nc.tensor.matmul(dst, agg_t[:, q * P:(q + 1) * P], w_scaled[:, 1, :], start=False, stop=False)
                    last = nc.tensor.matmul(dst, one_row[:, :], bias_row[:, :], start=False, stop=True)
                last.then_inc(final_written, 1)

            rounds_done = pe.alloc_register("pe_rounds_done")
            pe.reg_mov(rounds_done, 0)

            pe.wait_ge(basics_made, 8)
            for n in range(TURNS):
                turn_mask(0, 0, n)
            pe.wait_ge(basics_made, 11)
            for k in range(K):
                cutoff(0, TURNS, k)
            pe.wait_ge(consts_made, 4)
            for k in range(K):
                ranks(TURNS + K, TURNS, k)
            turn_h(0, True)
            pe.wait_ge(lo_made, 1)
            for use in (0, 1):
                pick_pair(0, use, 0)
            for n in range(TURNS):
                turn_mask(1, FIRST_RING - TURNS, n)
            for use in (2, 3):
                pick_pair(0, use, 0)

            def step(it, u):
                g = g_of(it, u)
                at = ring_of(it, u)
                more = not at_end(it, u, 1)
                slot = (u // PER_BATCH) % 2
                next_slot = ((u + 1) // PER_BATCH) % 2
                new_batch = more and u % PER_BATCH == PER_BATCH - 1
                done = pe.snap(rounds_done)
                for use in range(PAIRS, USES):
                    pick_pair(g, use, slot)
                    for i in (0, 1):
                        if 0 <= use - LATE_USE < PAIRS:
                            late_ranks(g, at + LATE_AT, 2 * (use - LATE_USE) + i)
                        if 0 <= use - CUT_USE < PAIRS and more:
                            cutoff(g + 1, at + CUT_AT, 2 * (use - CUT_USE) + i)
                        if 0 <= use - RANK_USE < PAIRS and more:
                            ranks(at + RANK_AT, at + CUT_AT, 2 * (use - RANK_USE) + i)
                    if use == LATE_USE + PAIRS - 1:
                        count(g, u % 2)
                if new_batch:
                    turn_h(batch_of(it, u + 1), False)
                pe.wait_ge(rounds_known, 1)
                pe.wait_ge(rounds_known, g + 1)
                n = pe.value_load(late_rounds[0:1, u % 2:u % 2 + 1], min_val=1, max_val=NEIGHBOURS)
                with pe.Fori(0, n) as r:
                    for s in range(2):
                        pe.wait_ge(picked_read, (g + 1) * READ - 1 + s)
                        pe.wait_ge(late_hot_made[s], done + (r + (g + 1)))
                        pe.wait_ge(late_read[s], done + r + 1)
                        for k in range(s * HALF, (s + 1) * HALF):
                            last = pick(picked[s][:, 0, :], k, late_hot[:, k, :], slot, k == s * HALF, k == (s + 1) * HALF - 1)
                        last.then_inc(late_written[s], 1)
                pe.reg_add(rounds_done, rounds_done, n)
                if more:
                    done = pe.snap(rounds_done)
                    if new_batch:
                        pe.wait_ge(lo_made, batch_of(it, u + 1) + 1)
                    for use in (0, 1):
                        pe.wait_ge(late_read[use], done + 1)
                        pick_pair(g + 1, use, next_slot)
                if not at_end(it, u, 2):
                    for k in (0, 1):
                        turn_mask(g + 2, at + TURN_AT, k)
                if more:
                    pick_pair(g + 1, 2, next_slot)
                project(g, it, u, new_batch)
                if more:
                    pick_pair(g + 1, 3, next_slot)
                if not at_end(it, u, 2):
                    for k in (2, 3):
                        turn_mask(g + 2, at + TURN_AT, k)

            over_groups(pe, step)

        @block.vector
        def _(dve):
            def make_mask(slot, loaded, turned):
                dve.wait_ge(adj_loaded[slot], loaded)
                if turned is not None:
                    dve.wait_ge(ring_written, turned)
                nc.vector.tensor_scalar(mask[:, :, :].rearrange("p q n -> p (q n)"), adj_in[:, slot, :], 0.0, None,
                                        ALU.not_equal).then_inc(mask_made, 1)

            def moments_of(batch):
                dve.wait_ge(x_loaded, 16 * batch + 16)
                for k in range(K):
                    nc.vector.bn_stats(stats[:, k, :], x_in[:, k, :]).then_inc(stats_made, 1)
                dve.wait_ge(stats_made, K * (batch + 1))
                nc.vector.memset(held[:, 3:4], 0.0)
                for k in range(K):
                    nc.vector.bn_aggr(moments[:, k, :], stats[:, k, :]).then_inc(moments_made, 1)

            def normalize(batch):
                dve.wait_ge(spread_made, batch + 1)
                nc.vector.reciprocal(gain[:, :], spread[:, :]).then_inc(gain_made, 1)
                dve.wait_ge(gain_made, 2 * batch + 1)
                nc.vector.tensor_scalar(gain[:, :], gain[:, :], SCALE, None, ALU.mult).then_inc(gain_made, 1)
                dve.wait_ge(gain_made, 2 * batch + 2)
                for k in range(K):
                    last = nc.vector.tensor_scalar(h32[:, k, :], x_in[:, k, :], moments[:, k, 0:1], gain[:, k:k + 1],
                                                   ALU.subtract, ALU.mult)
                last.then_inc(normed_made, 1)

            def make_hot(t, s):
                nc.vector.tensor_scalar(hot[:, (t - 1) % 3, :, :], rank[:, s, :, :], float(t), None,
                                        ALU.is_equal).then_inc(hot_made, 1)

            def find_late(s, ranked):
                dve.wait_ge(ring_read, ranked)
                nc.vector.tensor_scalar(late[:, :, :], rank[:, s, :, :], float(BASE), None, ALU.is_gt).then_inc(late_made, 1)

            def count_rounds(g, s):
                dve.wait_ge(count_written, g + 1)
                nc.vector.tensor_reduce(late_most[:, :], side[:, :], AX.X, ALU.max).then_inc(late_reduced, 1)
                dve.wait_ge(late_reduced, g + 1)
                nc.vector.tensor_scalar(late_rounds[:, s:s + 1], late_most[:, :], 1.0, None, ALU.max).then_inc(rounds_known, 1)

            def take_pair(g, use):
                s = use % 2
                if use < PAIRS:
                    dve.wait_ge(picked_copied, 2 * g + s + 1)
                dve.wait_ge(picked_written, g * USES + use + 1)
                nc.vector.tensor_tensor(best[:, s, :, :], picked[s][:, :, :], best[:, s, :, :],
                                        ALU.max).then_inc(picked_read, 1)

            def make_late_hot(i, which):
                part = slice(i * HALF, (i + 1) * HALF)
                nc.vector.tensor_scalar(late_hot[:, part, :], late_rank[:, part, :], which, None,
                                        ALU.is_equal).then_inc(late_hot_made[i], 1)

            def finish_group(g, s, loaded):
                dve.wait_ge(final_written, g + 1)
                dve.wait_ge(xres_loaded[s], loaded)
                nc.vector.scalar_tensor_tensor(out=result[:, s, :], in0=final[:, :], scalar=0.0, in1=xres[:, s, :],
                                               op0=ALU.max, op1=ALU.add).then_inc(result_made, 1)

            rounds_done = dve.alloc_register("dve_rounds_done")
            dve.reg_mov(rounds_done, 0)
            for i, opened in enumerate((result_made, late_read[0], late_read[1])):
                nc.vector.memset(held[:, i:i + 1], 0.0).then_inc(opened, 1)
            moments_of(0)
            make_mask(0, 16, None)
            normalize(0)
            dve.wait_ge(basics_made, 11)
            nc.vector.tensor_copy(numbers[:, :], numbers_i[:, :]).then_inc(consts_made, 1)
            nc.vector.scalar_tensor_tensor(out=rank_w[:, :], in0=eye[:, :], scalar=BIG, in1=upto[:, :], op0=ALU.mult,
                                           op1=ALU.add).then_inc(consts_made, 1)
            nc.vector.tensor_scalar(minus_w[:, :], eye[:, :], -BIG, None, ALU.mult).then_inc(consts_made, 1)
            dve.wait_ge(weights_loaded, 32)
            nc.vector.tensor_scalar(w_scaled[:, :, :], w_in[:, :, :], 1.0 / SCALE, None, ALU.mult).then_inc(consts_made, 1)
            make_mask(1, 16, TURNS)
            find_late(0, FIRST_RING - TURNS)
            make_hot(1, 0)
            make_hot(2, 0)
            take_pair(0, 2)
            make_mask(0, 32, FIRST_RING)
            take_pair(0, 3)
            make_hot(3, 0)

            def step(it, u):
                g, s = g_of(it, u), u % 2
                at = ring_of(it, u)
                more = not at_end(it, u, 1)
                new_batch = more and u % PER_BATCH == PER_BATCH - 1
                batch = batch_of(it, u + 1)

                for use in range(PAIRS, USES):
                    t, p = use // PAIRS, use % PAIRS
                    take_pair(g, use)
                    if use in (5, 9):
                        make_hot(use // PAIRS + 3, s)
                    if use == COUNT_USE:
                        count_rounds(g, s)
                    if use == COUNT_USE + 3:
                        dve.wait_ge(ring_read, at + CUT_AT)
                        for i in range(2):
                            make_late_hot(i, numbers[:, 1:2])
                    if use == MOMENTS_USE and new_batch:
                        moments_of(batch)
                    if use == NORMAL_USE and new_batch:
                        normalize(batch)
                    if use == RANK_USE + PAIRS + 1 and more:
                        find_late(1 - s, at + TURN_AT)

                if more:
                    make_hot(1, 1 - s)
                done = dve.snap(rounds_done)
                dve.wait_ge(rounds_known, 1)
                dve.wait_ge(rounds_known, g + 1)
                n = dve.value_load(late_rounds[0:1, s:s + 1], min_val=1, max_val=NEIGHBOURS)
                with dve.Fori(0, n) as r:
                    for i in range(2):
                        dve.wait_ge(late_written[i], done + r + 1)
                        nc.vector.tensor_tensor(best[:, i, 0, :], picked[i][:, 0, :], best[:, i, 0, :],
                                                ALU.max).then_inc(late_read[i], 1)
                        make_late_hot(i, numbers[:, bass.ds(r + 2, 1)])
                dve.reg_add(rounds_done, rounds_done, n)
                done = dve.snap(rounds_done)
                for i in range(2):
                    dve.wait_ge(late_read[i], done + 1)
                nc.vector.tensor_tensor(fold[:, :, :], best[:, 0, :, :], best[:, 1, :, :], ALU.max).then_inc(fold_step, 1)
                dve.wait_ge(fold_step, g + 1)
                nc.vector.tensor_tensor(agg_t[:, :], fold[:, 0, :], fold[:, 1, :], ALU.max).then_inc(agg_made, 1)
                if more:
                    make_hot(2, 1 - s)
                    take_pair(g + 1, 2)
                    make_hot(3, 1 - s)
                finish_group(g, s, 16 * (it * (UNROLL // 2) + u // 2 + 1))
                if more:
                    take_pair(g + 1, 3)
                if not at_end(it, u, 3):
                    make_mask((u + 3) % 2, 16 * (it * (UNROLL // 2) + (u + 3) // 2 + 1), at + RING)

            over_groups(dve, step)


_INS = ["x", "adj", "L0_gnn_W", "L0_gnn_b"]


def kernel(**inputs):
    import numpy as _np
    import concourse.bacc as _bacc
    from concourse import mybir as _mybir
    from concourse.bass_utils import run_bass_kernel_spmd as _run

    nc = _bacc.Bacc("TRN2", target_bir_lowering=False, num_devices=1)
    arrays, args = {}, []
    for name in _INS:
        a = _np.ascontiguousarray(inputs[name])
        arrays[f"in_{name}_dram"] = a
        args.append(nc.dram_tensor(f"in_{name}_dram", a.shape, _mybir.dt.from_np(a.dtype), kind="ExternalInput").ap())
    shape = inputs["x"].shape
    args.append(nc.dram_tensor("out_0_dram", shape, _mybir.dt.float32, kind="ExternalOutput").ap())
    build(nc, *args)
    r = _run(nc, [arrays], core_ids=[0])
    return r.results[0]["out_0_dram"]
```

```python
from contextlib import ExitStack

import concourse.bass as bass
from concourse import mybir

F32 = mybir.dt.float32
F16 = mybir.dt.float16
BF16 = mybir.dt.bfloat16
I32 = mybir.dt.int32
ALU = mybir.AluOpType
ACT = mybir.ActivationFunctionType
AX = mybir.AxisListType

P = 128
NEIGHBOURS = 25
BASE = 5
EPS = 1e-5
SCALE = 4096.0
BIG = 128.0


def build(nc, x, adj, W, b, out):
    B, N, C = x.shape
    K = N // P
    ROWS = 512
    Q = ROWS // P
    GROUPS = B * N // ROWS
    PER_BATCH = N // ROWS
    UNROLL = 2 * PER_BATCH
    ITERS = GROUPS // UNROLL
    PAIRS = K // 2
    HALF = K // 2
    USES = BASE * PAIRS
    READ = USES - 2

    def spread_over(first, last):
        return [[k for k in range(K) if use == first + k * (last - first + 1) // K] for use in range(USES)]

    LOWER_WITH, LATE_WITH, RANK_WITH = spread_over(4, 5), spread_over(6, 9), spread_over(12, 17)
    MASK_USES, LATE_HOT_USES, COUNT_USE, SIGN_USES = (7, 10, 12, 18), (13, 15), 10, (16, 17, 18, 19)
    PAST_USES = (8, 9, 11, 13)
    STATS_USES, MOMENTS_USE, SPREAD_USE, GAIN_USE, RELU_USE = (5, 6), 7, 9, 11, 15
    TURNS = K // 2
    FIRST_RING = 2 * TURNS + K
    RING = 2 * K + TURNS
    LATE_AT, RANK_AT, TURN_AT = 0, K, 2 * K
    assert C == P and K == 8 and PER_BATCH == 2 and BASE >= 5
    assert RING % 2 == 0 and FIRST_RING % 2 == 0

    adj_v = adj.rearrange("b (h p q) j -> (b h) p (q j)", p=P, q=Q)
    xres_v = x.rearrange("b (h p q) c -> (b h) p (q c)", p=P, q=Q)
    out_v = out.rearrange("b (h p q) c -> (b h) p (q c)", p=P, q=Q)
    x_v = x.rearrange("b (p k) c -> b p (k c)", k=K)

    with ExitStack() as ctx:
        def sb(name, shape, dt):
            return ctx.enter_context(nc.sbuf_tensor(name, shape, dt))

        def psum(name, shape, dt):
            return ctx.enter_context(nc.psum_tensor(name, shape, dt))

        def sem(name):
            return ctx.enter_context(nc.semaphore(name))

        ones = sb("ones", [P, P], BF16)
        eye = sb("eye", [P, P], BF16)
        eye32 = sb("eye32", [P, P], F32)
        upto = sb("upto", [P, P], BF16)
        before = sb("before", [P, P], BF16)
        rank_w = sb("rank_w", [P, P], BF16)
        minus_w = sb("minus_w", [P, P], BF16)
        numbers = sb("numbers", [P, 32], F32)
        numbers_i = sb("numbers_i", [P, 32], I32)
        half_w = sb("half_w", [P, P], BF16)
        half_ones = sb("half_ones", [P, P], BF16)
        late_bias = sb("late_bias", [P, K], F32)
        late_bias_i = sb("late_bias_i", [P, K], I32)
        bias_late = sb("bias_late", [P, 1], F32)
        bias_cut = sb("bias_cut", [P, 1], F32)
        bias_big = sb("bias_big", [P, 1], F32)
        bias_eps = sb("bias_eps", [P, 1], F32)
        bias_in = sb("bias_in", [3, C], F32)
        bias_part = sb("bias_part", [3, 3, C], BF16)
        bias_rest = sb("bias_rest", [3, 2, C], F32)
        bias_sum = sb("bias_sum", [3, 3, C], BF16)
        bias_parts = sb("bias_parts", [3, Q * C], BF16)
        w_in = sb("w_in", [P, 2, C], F32)
        w_scaled = sb("w_scaled", [P, 2, C], F32)
        adj_in = sb("adj_in", [P, 2, Q * N], I32)
        mask = sb("mask", [P, Q, N], BF16)
        mask_t = sb("mask_t", [P, K, ROWS], BF16)
        lower = sb("lower", [P, ROWS], F16)
        prefix = sb("prefix", [P, K, ROWS], F16)
        past = sb("past", [P, K, ROWS], BF16)
        rank = sb("rank", [P, 2, K, ROWS], BF16)
        late = sb("late", [P, K, ROWS], BF16)
        late_sum = sb("late_sum", [P, K - 1, ROWS], BF16)
        late_rank = sb("late_rank", [P, K, ROWS], BF16)
        late_most = sb("late_most", [P, 1], F32)
        late_rounds = sb("late_rounds", [P, 2], I32)
        hot = sb("hot", [P, 3, K, ROWS], F16)
        late_hot = sb("late_hot", [P, K, ROWS], F16)
        x_in = sb("x_in", [P, K, C], F32)
        stats = sb("stats", [P, K, 6], F32)
        moments = sb("moments", [P, K, 2], F32)
        held = sb("held", [P, 4], F32)
        spread = sb("spread", [P, K], F32)
        gain = sb("gain", [P, K], F32)
        h32 = sb("h32", [P, K, C], F32)
        h_hi = sb("h_hi", [P, 2, K, C], F16)
        h_lo = sb("h_lo", [P, 2, K, C], F16)
        h_t = sb("h_t", [P, 2, N], F32)
        best = sb("best", [P, 2, 2, 2, ROWS], F32)
        agg_t = sb("agg_t", [P, ROWS], F32)
        xres = sb("xres", [P, 2, Q * C], F32)
        result = sb("result", [P, 2, Q * C], F32)

        picked = [psum(f"picked{s}", [P, 2, ROWS], F32) for s in range(2)]
        ring = [psum(f"ring{s}", [P, ROWS], F32) for s in range(2)]
        ring16 = [r[:, :].bitcast(BF16).rearrange("p (k r) -> p k r", k=2) for r in ring]
        side = psum("side", [P, ROWS], F32)
        final = psum("final", [P, ROWS], F32)

        adj_loaded = [sem(f"adj_loaded{s}") for s in range(2)]
        xres_loaded = [sem(f"xres_loaded{s}") for s in range(2)]
        stored = [sem(f"stored{s}") for s in range(2)]
        x_loaded = sem("x_loaded")
        weights_loaded = sem("weights_loaded")
        bias_step = sem("bias_step")
        basics_made = sem("basics_made")
        consts_made = sem("consts_made")
        mask_made = sem("mask_made")
        ring_written = sem("ring_written")
        lower_written = sem("lower_written")
        lowered = sem("lowered")
        past_made = sem("past_made")
        ring_read = sem("ring_read")
        prefix_step = sem("prefix_step")
        late_made = sem("late_made")
        late_step = sem("late_step")
        count_written = sem("count_written")
        late_reduced = sem("late_reduced")
        rounds_known = sem("rounds_known")
        hot_made = sem("hot_made")
        picked_written = sem("picked_written")
        picked_copied = sem("picked_copied")
        picked_read = sem("picked_read")
        late_hot_made = [sem(f"late_hot_made{s}") for s in range(2)]
        late_written = [sem(f"late_written{s}") for s in range(2)]
        late_read = [sem(f"late_read{s}") for s in range(2)]
        fold_step = sem("fold_step")
        agg_made = sem("agg_made")
        final_written = sem("final_written")
        result_made = sem("result_made")
        stats_made = sem("stats_made")
        moments_made = sem("moments_made")
        spread_made = sem("spread_made")
        gain_made = sem("gain_made")
        centred = sem("centred")
        normed_made = sem("normed_made")
        h_made = sem("h_made")
        lo_made = sem("lo_made")
        h_written = sem("h_written")
        h_turned = sem("h_turned")

        block = ctx.enter_context(nc.Block())

        def over_groups(eng, step):
            with eng.Fori(0, ITERS - 1) as it:
                for u in range(UNROLL):
                    step(it, u)
            for u in range(UNROLL):
                step(ITERS - 1, u)

        def g_of(it, u):
            return it * UNROLL + u

        def batch_of(it, u):
            return it * (UNROLL // PER_BATCH) + u // PER_BATCH

        def at_end(it, u, ahead):
            return isinstance(it, int) and it * UNROLL + u + ahead >= GROUPS

        def ring_of(it, u):
            skipped = TURNS if at_end(it, u, 1) else 0
            return (it * UNROLL + u) * RING + FIRST_RING - skipped

        def class_sums(eng, engine, g):
            eng.wait_ge(lowered, g + 1)
            for k in range(K):
                if k:
                    eng.wait_ge(prefix_step, g * K + k)
                first = lower[:, :] if k == 0 else prefix[:, k - 1, :]
                engine.tensor_tensor(prefix[:, k, :], first, mask_t[:, k, :], ALU.add).then_inc(prefix_step, 1)

        def late_sums(eng, engine, g):
            for k in range(2, K + 1):
                if k == 2 or k % 2 == 1:
                    eng.wait_ge(late_made, g * PAIRS + (k + 1) // 2)
                if k > 2:
                    eng.wait_ge(late_step, g * (K - 1) + k - 2)
                first = late[:, 0, :] if k == 2 else late_sum[:, k - 3, :]
                engine.tensor_tensor(late_sum[:, k - 2, :], first, late[:, k - 1, :], ALU.add).then_inc(late_step, 1)

        @block.sync
        def _(sp):
            def load_adj(g, slot):
                sp.dma_start(adj_in[:, slot, :], adj_v[g]).then_inc(adj_loaded[slot], 16)

            def load_xres(g, slot):
                sp.dma_start(xres[:, slot, :], xres_v[g]).then_inc(xres_loaded[slot], 16)

            def load_x(batch):
                sp.dma_start(x_in[:, :, :].rearrange("p k c -> p (k c)"), x_v[batch]).then_inc(x_loaded, 16)

            load_adj(0, 0)
            load_x(0)
            load_adj(1, 1)
            sp.dma_start(w_in[:, :, :], W.rearrange("(s p) n -> p s n", p=P)).then_inc(weights_loaded, 16)
            for i in range(3):
                sp.dma_start(bias_in[i:i + 1, :], b.rearrange("(a n) -> a n", a=1)).then_inc(weights_loaded, 16)
            load_xres(0, 0)
            for g in (0, 1):
                sp.wait_ge(mask_made, Q * (g + 1))
                load_adj(g + 2, g)

            def step(it, u):
                g = g_of(it, u)
                if not at_end(it, u, 1):
                    sp.wait_ge(result_made, g + 1)
                    load_xres(g + 1, (u + 1) % 2)
                if u % PER_BATCH == 0 and not at_end(it, u, PER_BATCH):
                    sp.wait_ge(normed_made, batch_of(it, u) + 1)
                    load_x(batch_of(it, u) + 1)
                sp.wait_ge(result_made, g + 2)
                sp.dma_start(out_v[g], result[:, u % 2, :]).then_inc(stored[u % 2], 16)
                sp.wait_ge(stored[u % 2], 16 * (it * (UNROLL // 2) + u // 2 + 1))
                if not at_end(it, u, 4):
                    load_adj(g + 4, u % 2)

            over_groups(sp, step)

        @block.gpsimd
        def _(pool):
            nc.gpsimd.memset(ones[:, :], 1.0).then_inc(basics_made, 1)
            nc.gpsimd.memset(eye32[:, :], 1.0).then_inc(basics_made, 1)
            nc.gpsimd.iota(numbers_i[:, :], pattern=[[1, 32]], base=0, channel_multiplier=0).then_inc(basics_made, 1)
            nc.gpsimd.iota(late_bias_i[:, :], pattern=[[P, K]], base=1, channel_multiplier=1).then_inc(basics_made, 1)
            nc.gpsimd.memset(half_ones[:, :], 0.5).then_inc(basics_made, 1)
            nc.gpsimd.memset(bias_cut[:, :], -float(NEIGHBOURS)).then_inc(basics_made, 1)
            nc.gpsimd.memset(bias_big[:, :], -BIG).then_inc(basics_made, 1)
            nc.gpsimd.memset(bias_eps[:, :], EPS).then_inc(basics_made, 1)
            nc.gpsimd.memset(bias_late[:, :], -(BASE + 0.5)).then_inc(basics_made, 1)
            pool.wait_ge(basics_made, 9)
            line = dict(pattern=[[1, P]], channel_multiplier=-1, fill=0.0)
            nc.gpsimd.affine_select(out=eye[:, :], in_=ones[:, :], compare_op=ALU.is_equal, base=0, **line).then_inc(basics_made, 1)
            nc.gpsimd.affine_select(out=upto[:, :], in_=ones[:, :], compare_op=ALU.is_ge, base=0, **line).then_inc(basics_made, 1)
            nc.gpsimd.affine_select(out=before[:, :], in_=ones[:, :], compare_op=ALU.is_gt, base=0, **line).then_inc(basics_made, 1)
            nc.gpsimd.affine_select(out=eye32[:, :], in_=eye32[:, :], compare_op=ALU.is_equal, base=0, **line).then_inc(basics_made, 1)

            def low_part(batch, slot):
                pool.wait_ge(h_made, 2 * batch + 2)
                nc.gpsimd.tensor_tensor(h_lo[:, slot, :, :], h32[:, :, :], h_hi[:, slot, :, :], ALU.subtract).then_inc(lo_made, 1)

            def normalize(batch):
                pool.wait_ge(gain_made, 2 * batch + 2)
                mean = moments[:, :, 0:1].to_broadcast([P, K, C])
                nc.gpsimd.tensor_tensor(h32[:, :, :], x_in[:, :, :], mean, ALU.subtract).then_inc(centred, 1)
                pool.wait_ge(centred, batch + 1)
                scale = gain[:, :].unsqueeze(2).to_broadcast([P, K, C])
                nc.gpsimd.tensor_tensor(h32[:, :, :], h32[:, :, :], scale, ALU.mult).then_inc(normed_made, 1)

            normalize(0)
            low_part(0, 0)

            def step(it, u):
                g = g_of(it, u)
                if not at_end(it, u, 1):
                    class_sums(pool, nc.gpsimd, g + 1)
                    if u % PER_BATCH == PER_BATCH - 1:
                        normalize(batch_of(it, u + 1))
                        low_part(batch_of(it, u + 1), ((u + 1) // PER_BATCH) % 2)
                    late_sums(pool, nc.gpsimd, g + 1)

            over_groups(pool, step)

        @block.scalar
        def _(act):
            act.wait_ge(basics_made, 10)

            def turned_mask(at, n):
                act.wait_ge(ring_written, at + n + 1)
                nc.scalar.activation(mask_t[:, 2 * n:2 * n + 2, :], ring16[n % 2], ACT.Abs).then_inc(ring_read, 1)

            def make_mask(q, slot, loaded, turned):
                act.wait_ge(adj_loaded[slot], loaded)
                act.wait_ge(ring_written, turned)
                nc.scalar.activation(mask[:, q, :], adj_in[:, slot, q * N:(q + 1) * N], ACT.Sign).then_inc(mask_made, 1)

            def stage(at, k, dst, bias):
                act.wait_ge(ring_written, at + k + 1)
                nc.scalar.activation(dst[:, k, :], ring[k % 2][:, :], ACT.Relu, bias=bias).then_inc(ring_read, 1)

            def copy_lower(g):
                act.wait_ge(lower_written, g + 1)
                nc.scalar.copy(lower[:, :], side[:, :]).then_inc(lowered, 1)

            def find_past(g, p):
                act.wait_ge(prefix_step, g * K + 2 * p + 2)
                nc.scalar.activation(past[:, 2 * p:2 * p + 2, :], prefix[:, 2 * p:2 * p + 2, :], ACT.Relu,
                                     bias=bias_cut[:, 0:1]).then_inc(past_made, 1)

            def find_late(p, s, ranked):
                act.wait_ge(ring_read, ranked)
                nc.scalar.activation(late[:, 2 * p:2 * p + 2, :], rank[:, s, 2 * p:2 * p + 2, :], ACT.Sign,
                                     bias=bias_late[:, 0:1]).then_inc(late_made, 1)

            def spreads(batch):
                act.wait_ge(moments_made, K * batch + K)
                nc.scalar.activation(spread[:, :], moments[:, :, 1], ACT.Sqrt, bias=bias_eps[:, 0:1]).then_inc(spread_made, 1)

            def relu_parts(batch, slot):
                act.wait_ge(normed_made, batch + 1)
                nc.scalar.activation(h_hi[:, slot, :, :], h32[:, :, :], ACT.Relu).then_inc(h_made, 1)
                act.wait_ge(h_made, 2 * batch + 1)
                nc.scalar.activation(h32[:, :, :], h32[:, :, :], ACT.Relu).then_inc(h_made, 1)

            def turned_h(batch, slot):
                dst = h_t[:, slot, :].rearrange("c (a k) -> c k a", k=K)
                for n, bank in enumerate((side, final)):
                    act.wait_ge(h_written, 2 * batch + n + 1)
                    nc.scalar.copy(dst[:, 4 * n:4 * n + 4, :], bank[:, :].rearrange("c (k a) -> c k a", k=4)).then_inc(h_turned, 1)

            def first_maxima(g, s, half):
                act.wait_ge(picked_written, g * USES + s + 1)
                nc.scalar.copy(best[:, half, s, :, :], picked[s][:, :, :]).then_inc(picked_copied, 1)

            for n in range(TURNS):
                turned_mask(0, n)
            copy_lower(0)
            for p in range(PAIRS):
                find_past(0, p)
            spreads(0)
            relu_parts(0, 0)
            for k in range(K):
                stage(TURNS, k, rank[:, 0], bias_big[:, 0:1])
            turned_h(0, 0)
            find_late(0, 0, FIRST_RING - TURNS)
            act.wait_ge(consts_made, 5)
            for s in range(2):
                first_maxima(0, s, 0)
            for p in range(1, PAIRS):
                find_late(p, 0, FIRST_RING - TURNS)
            for n in (0, 1):
                turned_mask(FIRST_RING - TURNS, n)

            def step(it, u):
                g = g_of(it, u)
                at = ring_of(it, u)
                more = not at_end(it, u, 1)
                new_batch = more and u % PER_BATCH == PER_BATCH - 1
                batch, slot = batch_of(it, u + 1), ((u + 1) // PER_BATCH) % 2
                for use in range(PAIRS, USES):
                    if use == PAIRS and more:
                        for k in (2, 3):
                            turned_mask(at - TURNS, k)
                    if K - 1 in LOWER_WITH[use] and more:
                        copy_lower(g + 1)
                    for k in LATE_WITH[use]:
                        stage(at + LATE_AT, k, late_rank, late_bias[:, k:k + 1])
                    if use in PAST_USES and more:
                        find_past(g + 1, PAST_USES.index(use))
                    for k in RANK_WITH[use] if more else []:
                        stage(at + RANK_AT, k, rank[:, (u + 1) % 2], bias_big[:, 0:1])
                    if use in MASK_USES and not at_end(it, u, 2):
                        make_mask(MASK_USES.index(use), u % 2, 16 * (it * (UNROLL // 2) + u // 2 + 2), at)
                    if use == SPREAD_USE and new_batch:
                        spreads(batch)
                    if use == RELU_USE and new_batch:
                        relu_parts(batch, slot)
                    if use in SIGN_USES and more:
                        p = SIGN_USES.index(use)
                        find_late(p, (u + 1) % 2, at + RANK_AT + 2 * p + 2)
                if new_batch:
                    turned_h(batch, slot)
                if more:
                    for s in range(2):
                        first_maxima(g + 1, s, (u + 1) % 2)
                if not at_end(it, u, 2):
                    for k in (0, 1):
                        turned_mask(at + TURN_AT, k)

            over_groups(act, step)

        @block.tensor
        def _(pe):
            def take(at):
                if not isinstance(at, int) or at >= 2:
                    pe.wait_ge(ring_read, at - 1)

            def turn_mask(g, at, n):
                if n == 0:
                    pe.wait_ge(mask_made, Q * (g + 1))
                take(at + n)
                for j in range(2):
                    for q in range(Q):
                        last = nc.tensor.transpose(ring16[n % 2][:, j, q * P:(q + 1) * P], mask[:, q, 2 * n + j::K], eye[:, :])
                last.then_inc(ring_written, 1)

            def accumulate(at, k, terms):
                take(at + k)
                for i, (w, m) in enumerate(terms):
                    last = nc.tensor.matmul(ring[k % 2][:, :], w[:, :], m, start=(i == 0), stop=(i == len(terms) - 1))
                last.then_inc(ring_written, 1)

            def lower_sums(g, parity, turned, classes):
                if classes[0] == 0 and parity == 1:
                    pe.wait_ge(h_turned, g + 1)
                if classes[0] == 0 and parity == 0:
                    pe.wait_ge(rounds_known, g - 1)
                for k in classes:
                    if k % 2 == 0:
                        pe.wait_ge(ring_read, turned + k // 2 + 1)
                    last = nc.tensor.matmul(side[:, :], before[:, :], mask_t[:, k, :], start=(k == 0), stop=(k == K - 1))
                if classes[-1] == K - 1:
                    last.then_inc(lower_written, 1)

            def ranks(g, at, k):
                pe.wait_ge(past_made, g * PAIRS + k // 2 + 1)
                accumulate(at, k, [(rank_w, mask_t[:, k, :]), (minus_w, past[:, k, :])])

            def late_ranks(g, at, k):
                if k == 0:
                    pe.wait_ge(late_step, (g + 1) * (K - 1))
                terms = [(half_w, late[:, k, :])]
                if k:
                    terms.append((half_ones, late[:, 0, :] if k == 1 else late_sum[:, k - 2, :]))
                accumulate(at, k, terms)

            def count(g, more):
                if more:
                    pe.wait_ge(lowered, g + 2)
                else:
                    pe.wait_ge(rounds_known, g)
                nc.tensor.matmul(side[:, :], half_ones[:, :], late_sum[:, K - 2, :], start=True, stop=True).then_inc(count_written, 1)

            def turn_h(batch, first):
                pe.wait_ge(h_made, 2 * batch + 2)
                for n, bank in enumerate((side, final)):
                    if not first:
                        pe.wait_ge((rounds_known, result_made)[n], 2 * batch)
                    for j in range(4):
                        last = nc.tensor.transpose(bank[:, j * P:(j + 1) * P], h32[:, 4 * n + j, :], eye32[:, :])
                    last.then_inc(h_written, 1)

            def pick(dst, k, onehot, slot, start, stop):
                nc.tensor.matmul(dst, h_hi[:, slot, k, :], onehot, start=start, stop=False)
                return nc.tensor.matmul(dst, h_lo[:, slot, k, :], onehot, start=False, stop=stop)

            def pick_pair(g, use, slot):
                t, p = use // PAIRS, use % PAIRS
                if p == 0:
                    pe.wait_ge(hot_made, g * BASE + t + 1)
                if use in (2, 3):
                    pe.wait_ge(picked_copied, g * 2 + use - 1)
                if use > 3:
                    pe.wait_ge(picked_read, g * READ + use - 3)
                for j in range(2):
                    last = pick(picked[p % 2][:, j, :], 2 * p + j, hot[:, t % 3, 2 * p + j, :], slot, True, True)
                last.then_inc(picked_written, 1)

            def project(g, it, u, new_batch):
                slot = (u // PER_BATCH) % 2
                pe.wait_ge(result_made, g + 1)
                if u % PER_BATCH == 0:
                    pe.wait_ge(h_turned, 2 * batch_of(it, u) + 2)
                if new_batch:
                    pe.wait_ge(h_turned, 2 * batch_of(it, u + 1) + 2)
                first = (u % PER_BATCH) * ROWS
                nc.tensor.matmul(final[:, :], ones[0:3, :], bias_parts[:, :], start=True, stop=False)
                for q in range(Q):
                    nc.tensor.matmul(final[:, q * C:(q + 1) * C], h_t[:, slot, first + q:first + ROWS:Q], w_scaled[:, 0, :],
                                     start=False, stop=False)
                pe.wait_ge(agg_made, g + 1)
                for q in range(Q):
                    last = nc.tensor.matmul(final[:, q * C:(q + 1) * C], agg_t[:, q * P:(q + 1) * P], w_scaled[:, 1, :],
                                            start=False, stop=(q == Q - 1))
                last.then_inc(final_written, 1)

            rounds_done = pe.alloc_register("pe_rounds_done")
            pe.reg_mov(rounds_done, 0)

            pe.wait_ge(basics_made, 10)
            for n in range(TURNS):
                turn_mask(0, 0, n)
            pe.wait_ge(basics_made, 13)
            lower_sums(0, None, 0, range(K))
            pe.wait_ge(consts_made, 5)
            for k in range(K):
                ranks(0, TURNS, k)
            turn_h(0, True)
            pe.wait_ge(lo_made, 1)
            for use in range(PAIRS):
                pick_pair(0, use, 0)
            for n in (0, 1):
                turn_mask(1, FIRST_RING - TURNS, n)

            pe.wait_ge(consts_made, 10)

            def step(it, u):
                g = g_of(it, u)
                at = ring_of(it, u)
                more = not at_end(it, u, 1)
                slot = (u // PER_BATCH) % 2
                next_slot = ((u + 1) // PER_BATCH) % 2
                new_batch = more and u % PER_BATCH == PER_BATCH - 1
                done = pe.snap(rounds_done)
                for use in range(PAIRS, USES):
                    pick_pair(g, use, slot)
                    if use == PAIRS and more:
                        for k in (2, 3):
                            turn_mask(g + 1, at - TURNS, k)
                    if LOWER_WITH[use] and more:
                        lower_sums(g + 1, (u + 1) % 2, at - TURNS, LOWER_WITH[use])
                    for k in LATE_WITH[use]:
                        late_ranks(g, at + LATE_AT, k)
                    if K - 1 in LATE_WITH[use]:
                        count(g, more)
                    for k in RANK_WITH[use] if more else []:
                        ranks(g + 1, at + RANK_AT, k)
                if new_batch:
                    turn_h(batch_of(it, u + 1), False)
                pe.wait_ge(rounds_known, 1)
                pe.wait_ge(rounds_known, g + 1)
                n = pe.value_load(late_rounds[0:1, u % 2:u % 2 + 1], min_val=1, max_val=NEIGHBOURS)
                with pe.Fori(0, n) as r:
                    for s in range(2):
                        pe.wait_ge(picked_read, (g + 1) * READ - 1 + s)
                        pe.wait_ge(late_hot_made[s], done + (r + (g + 1)))
                        pe.wait_ge(late_read[s], done + r + 1)
                        for k in range(s * HALF, (s + 1) * HALF):
                            last = pick(picked[s][:, 0, :], k, late_hot[:, k, :], slot, k == s * HALF, k == (s + 1) * HALF - 1)
                        last.then_inc(late_written[s], 1)
                pe.reg_add(rounds_done, rounds_done, n)
                if more:
                    done = pe.snap(rounds_done)
                    if new_batch:
                        pe.wait_ge(lo_made, batch_of(it, u + 1) + 1)
                    for use in (0, 1):
                        pe.wait_ge(late_read[use], done + 1)
                        pick_pair(g + 1, use, next_slot)
                if not at_end(it, u, 2):
                    turn_mask(g + 2, at + TURN_AT, 0)
                if more:
                    pick_pair(g + 1, 2, next_slot)
                if not at_end(it, u, 2):
                    turn_mask(g + 2, at + TURN_AT, 1)
                if more:
                    pick_pair(g + 1, 3, next_slot)
                project(g, it, u, new_batch)

            over_groups(pe, step)

        @block.vector
        def _(dve):
            def make_mask(q, slot, loaded, turned):
                dve.wait_ge(adj_loaded[slot], loaded)
                if turned is not None:
                    dve.wait_ge(ring_written, turned)
                nc.vector.tensor_scalar(mask[:, q, :], adj_in[:, slot, q * N:(q + 1) * N], 0.0, None,
                                        ALU.not_equal).then_inc(mask_made, 1)

            def stats_of(batch, classes):
                dve.wait_ge(x_loaded, 16 * batch + 16)
                for k in classes:
                    nc.vector.bn_stats(stats[:, k, :], x_in[:, k, :]).then_inc(stats_made, 1)

            def moments_of(batch):
                dve.wait_ge(stats_made, K * (batch + 1))
                nc.vector.memset(held[:, 3:4], 0.0)
                for k in range(K):
                    nc.vector.bn_aggr(moments[:, k, :], stats[:, k, :]).then_inc(moments_made, 1)

            def make_gain(batch):
                dve.wait_ge(spread_made, batch + 1)
                nc.vector.reciprocal(gain[:, :], spread[:, :]).then_inc(gain_made, 1)
                dve.wait_ge(gain_made, 2 * batch + 1)
                nc.vector.tensor_scalar(gain[:, :], gain[:, :], SCALE, None, ALU.mult).then_inc(gain_made, 1)

            def make_hot(t, s):
                nc.vector.tensor_scalar(hot[:, (t - 1) % 3, :, :], rank[:, s, :, :], float(t), None,
                                        ALU.is_equal).then_inc(hot_made, 1)

            def count_rounds(g, s):
                dve.wait_ge(count_written, g + 1)
                nc.vector.tensor_reduce(late_most[:, :], side[:, :], AX.X, ALU.max).then_inc(late_reduced, 1)
                dve.wait_ge(late_reduced, g + 1)
                nc.vector.tensor_scalar(late_rounds[:, s:s + 1], late_most[:, :], K * P / 2, 1.0, ALU.add,
                                        ALU.max).then_inc(rounds_known, 1)

            def take_pair(g, use, half):
                s = use % 2
                if use < PAIRS:
                    dve.wait_ge(picked_copied, 2 * g + s + 1)
                dve.wait_ge(picked_written, g * USES + use + 1)
                nc.vector.tensor_tensor(best[:, half, s, :, :], picked[s][:, :, :], best[:, half, s, :, :],
                                        ALU.max).then_inc(picked_read, 1)

            def make_late_hot(i, which):
                part = slice(i * HALF, (i + 1) * HALF)
                nc.vector.tensor_scalar(late_hot[:, part, :], late_rank[:, part, :], which, None,
                                        ALU.is_equal).then_inc(late_hot_made[i], 1)

            def finish_group(g, s, loaded):
                dve.wait_ge(final_written, g + 1)
                dve.wait_ge(xres_loaded[s], loaded)
                nc.vector.scalar_tensor_tensor(out=result[:, s, :], in0=final[:, :], scalar=0.0, in1=xres[:, s, :],
                                               op0=ALU.max, op1=ALU.add).then_inc(result_made, 1)

            rounds_done = dve.alloc_register("dve_rounds_done")
            dve.reg_mov(rounds_done, 0)
            for i, opened in enumerate((result_made, late_read[0], late_read[1])):
                nc.vector.memset(held[:, i:i + 1], 0.0).then_inc(opened, 1)
            for q in range(Q):
                make_mask(q, 0, 16, None)
            stats_of(0, range(K))
            moments_of(0)
            dve.wait_ge(basics_made, 13)
            nc.vector.tensor_copy(numbers[:, :], numbers_i[:, :]).then_inc(consts_made, 1)
            nc.vector.scalar_tensor_tensor(out=rank_w[:, :], in0=eye[:, :], scalar=BIG, in1=upto[:, :], op0=ALU.mult,
                                           op1=ALU.add).then_inc(consts_made, 1)
            nc.vector.tensor_scalar(late_bias[:, :], late_bias_i[:, :], 0.5, -BIG / 2, ALU.mult, ALU.add).then_inc(consts_made, 1)
            dve.wait_ge(consts_made, 2)
            nc.vector.tensor_scalar(half_w[:, :], rank_w[:, :], 0.5, None, ALU.mult).then_inc(consts_made, 1)
            nc.vector.tensor_scalar(minus_w[:, :], eye[:, :], -BIG, None, ALU.mult).then_inc(consts_made, 1)
            class_sums(dve, nc.vector, 0)
            make_gain(0)
            for q in range(Q):
                make_mask(q, 1, 16, TURNS)
            dve.wait_ge(ring_read, FIRST_RING - TURNS)
            make_hot(1, 0)
            make_hot(2, 0)
            dve.wait_ge(weights_loaded, 64)
            nc.vector.tensor_scalar(w_scaled[:, :, :], w_in[:, :, :], 1.0 / SCALE, None, ALU.mult).then_inc(consts_made, 1)
            rest = bias_in
            for i in range(3):
                nc.vector.tensor_copy(bias_part[:, i, :], rest[:, :]).then_inc(bias_step, 1)
                dve.wait_ge(bias_step, 2 * i + 1)
                if i < 2:
                    nc.vector.tensor_tensor(bias_rest[:, i, :], rest[:, :], bias_part[:, i, :], ALU.subtract).then_inc(bias_step, 1)
                    rest = bias_rest[:, i, :]
                    dve.wait_ge(bias_step, 2 * i + 2)
            nc.vector.tensor_scalar(bias_sum[:, 0, :], bias_part[:, 0, :], eye32[0:3, 0:1], None, ALU.mult).then_inc(bias_step, 1)
            for i in (1, 2):
                dve.wait_ge(bias_step, 5 + i)
                nc.vector.scalar_tensor_tensor(out=bias_sum[:, i, :], in0=bias_part[:, i, :], scalar=eye32[0:3, i:i + 1],
                                               in1=bias_sum[:, i - 1, :], op0=ALU.mult, op1=ALU.add).then_inc(bias_step, 1)
            dve.wait_ge(bias_step, 8)
            for q in range(Q):
                nc.vector.tensor_copy(bias_parts[:, q * C:(q + 1) * C], bias_sum[:, 2, :]).then_inc(consts_made, 1)
            take_pair(0, 2, 0)
            make_hot(3, 0)
            take_pair(0, 3, 0)
            late_sums(dve, nc.vector, 0)

            def step(it, u):
                g, s = g_of(it, u), u % 2
                at = ring_of(it, u)
                more = not at_end(it, u, 1)
                new_batch = more and u % PER_BATCH == PER_BATCH - 1
                batch = batch_of(it, u + 1)

                for use in range(PAIRS, USES):
                    t, p = use // PAIRS, use % PAIRS
                    take_pair(g, use, s)
                    if use in (5, 9):
                        make_hot(use // PAIRS + 3, s)
                    if use == COUNT_USE:
                        count_rounds(g, s)
                    if use in LATE_HOT_USES:
                        dve.wait_ge(ring_read, at + RANK_AT)
                        make_late_hot(LATE_HOT_USES.index(use), numbers[:, 1:2])
                    if use in STATS_USES and new_batch:
                        half = STATS_USES.index(use)
                        stats_of(batch, range(half * HALF, (half + 1) * HALF))
                    if use == MOMENTS_USE and new_batch:
                        moments_of(batch)
                    if use == GAIN_USE and new_batch:
                        make_gain(batch)

                if more:
                    dve.wait_ge(ring_read, at + TURN_AT)
                    make_hot(1, 1 - s)
                done = dve.snap(rounds_done)
                dve.wait_ge(rounds_known, 1)
                dve.wait_ge(rounds_known, g + 1)
                n = dve.value_load(late_rounds[0:1, s:s + 1], min_val=1, max_val=NEIGHBOURS)
                with dve.Fori(0, n) as r:
                    for i in range(2):
                        dve.wait_ge(late_written[i], done + r + 1)
                        nc.vector.tensor_tensor(best[:, s, i, 0, :], picked[i][:, 0, :], best[:, s, i, 0, :],
                                                ALU.max).then_inc(late_read[i], 1)
                        make_late_hot(i, numbers[:, bass.ds(r + 2, 1)])
                dve.reg_add(rounds_done, rounds_done, n)
                done = dve.snap(rounds_done)
                for i in range(2):
                    dve.wait_ge(late_read[i], done + 1)
                nc.vector.tensor_tensor(best[:, s, 0, :, :], best[:, s, 0, :, :], best[:, s, 1, :, :], ALU.max).then_inc(fold_step, 1)
                dve.wait_ge(fold_step, g + 1)
                nc.vector.tensor_tensor(agg_t[:, :], best[:, s, 0, 0, :], best[:, s, 0, 1, :], ALU.max).then_inc(agg_made, 1)
                if more:
                    make_hot(2, 1 - s)
                    take_pair(g + 1, 2, 1 - s)
                    make_hot(3, 1 - s)
                if more:
                    take_pair(g + 1, 3, 1 - s)
                finish_group(g, s, 16 * (it * (UNROLL // 2) + u // 2 + 1))

            over_groups(dve, step)


_INS = ["x", "adj", "L0_gnn_W", "L0_gnn_b"]


def kernel(**inputs):
    import numpy as _np
    import concourse.bacc as _bacc
    from concourse import mybir as _mybir
    from concourse.bass_utils import run_bass_kernel_spmd as _run

    nc = _bacc.Bacc("TRN2", target_bir_lowering=False, num_devices=1)
    arrays, args = {}, []
    for name in _INS:
        a = _np.ascontiguousarray(inputs[name])
        arrays[f"in_{name}_dram"] = a
        args.append(nc.dram_tensor(f"in_{name}_dram", a.shape, _mybir.dt.from_np(a.dtype), kind="ExternalInput").ap())
    shape = inputs["x"].shape
    args.append(nc.dram_tensor("out_0_dram", shape, _mybir.dt.float32, kind="ExternalOutput").ap())
    build(nc, *args)
    r = _run(nc, [arrays], core_ids=[0])
    return r.results[0]["out_0_dram"]
```
